# Optimizing a Trainium2 kernel written in Bass

```python
import numpy as np
import jax
import jax.numpy as jnp

def _softmax(x, axis=-1):
    return jax.nn.softmax(x, axis=axis)

def _gelu(x):
    return jax.nn.gelu(x, approximate=True)

def _silu(x):
    return jax.nn.silu(x)

def _sigmoid(x):
    return jax.nn.sigmoid(x)

def _layernorm(x, axis=-1, eps=1e-05):
    m = jnp.mean(x, axis=axis, keepdims=True)
    v = jnp.var(x, axis=axis, keepdims=True)
    return (x - m) / jnp.sqrt(v + eps)

def _scatter_add(tgt, idx, src, axis=0):
    return tgt.at[idx].add(src)

def _segment_sum(src, seg, n):
    return jax.ops.segment_sum(src, seg, n)
kernel_name = 'mk_gnn_preln_d2_gnn_r64_73597c'

def setup_inputs(seed: int=0):
    np.random.seed(seed)
    _w = jnp.asarray

    def _rec_inputs():
        import jax
        import jax.numpy as jnp
        _gk = jax.random.key(seed)
        x = -0.000202 + 1 * jax.random.normal(jax.random.fold_in(_gk, 1), (100000, 128), jnp.float32)
        src = jax.random.randint(jax.random.fold_in(_gk, 2), (50000,), 0, 100000, jnp.int32)
        dst = jax.random.randint(jax.random.fold_in(_gk, 3), (50000,), 0, 100000, jnp.int32)
        _o = jnp.argsort(dst, stable=True)
        src = src[_o]
        dst = dst[_o]
        edge_type_200 = jax.random.randint(jax.random.fold_in(_gk, 13), (50000,), 0, 200, jnp.int32)
        return (x, src, dst, edge_type_200)
    x, src, dst, edge_type_200 = _rec_inputs()

    def _L0_gnn_setup():
        import jax, jax.numpy as jnp
        import numpy as np
        N = 50000
        E = 500000
        R = 200
        DIN = 128
        DREL = 128
        DOUT = 128
        SLOPE = 0.01
        key = jax.random.key(seed)
        ks = jax.random.split(key, 6)
        x = jax.random.normal(ks[0], (N, DIN), dtype=jnp.float32)
        relation_embedding = jax.random.normal(ks[1], (R, DREL), dtype=jnp.float32)
        edge_index = jax.random.randint(ks[2], (2, E), 0, N, dtype=jnp.int32)
        edge_type = jax.random.randint(ks[3], (E,), 0, R, dtype=jnp.int32)
        W1 = jax.random.normal(ks[4], (2 * DIN + DREL, DOUT), dtype=jnp.float32) * 0.05
        b1 = jnp.zeros((DOUT,), dtype=jnp.float32)
        w2 = jax.random.normal(ks[5], (DOUT,), dtype=jnp.float32) * 0.05
        return {'x': x, 'relation_embedding': relation_embedding, 'W1': W1, 'b1': b1, 'w2': w2, 'edge_index': edge_index, 'edge_type': edge_type}
    _L0_gnn_all = _L0_gnn_setup()
    _L0_gnn_in = {k: v for k, v in _L0_gnn_all.items() if k in ('relation_embedding', 'W1', 'b1', 'w2')}
    del _L0_gnn_all

    def _L1_gnn_setup():
        import jax, jax.numpy as jnp
        import numpy as np
        N_NODES = 100000
        N_EDGES = 25000
        D_FEAT = 128
        key = jax.random.key(seed)
        k1, k2, k3 = jax.random.split(key, 3)
        feats = jax.random.normal(k1, (N_NODES, D_FEAT), dtype=jnp.float32)
        src = jax.random.randint(k2, (N_EDGES,), 0, N_NODES, dtype=jnp.int64)
        dst = jax.random.randint(k3, (N_EDGES,), 0, N_NODES, dtype=jnp.int64)
        return {'feats': feats, 'src': src, 'dst': dst}
    _L1_gnn_all = _L1_gnn_setup()
    _L1_gnn_in = {k: v for k, v in _L1_gnn_all.items() if k in ()}
    del _L1_gnn_all
    return {'x': x, 'src': src, 'dst': dst, 'edge_type_200': edge_type_200, 'L0_gnn_relation_embedding': _L0_gnn_in['relation_embedding'], 'L0_gnn_W1': _L0_gnn_in['W1'], 'L0_gnn_b1': _L0_gnn_in['b1'], 'L0_gnn_w2': _L0_gnn_in['w2']}

def reference(x, src, dst, edge_type_200, L0_gnn_relation_embedding, L0_gnn_W1, L0_gnn_b1, L0_gnn_w2):
    import jax
    import jax.numpy as jnp

    def _L0_gnn_ref(x, relation_embedding, W1, b1, w2, edge_index, edge_type):
        import jax, jax.numpy as jnp
        import numpy as np
        N = 50000
        E = 500000
        R = 200
        DIN = 128
        DREL = 128
        DOUT = 128
        SLOPE = 0.01
        src, dst = (edge_index[0], edge_index[1])
        n = x.shape[0]
        triple = jnp.concatenate([x[src], x[dst], relation_embedding[edge_type]], axis=1)
        c = triple @ W1 + b1
        b = jax.nn.leaky_relu(c @ w2, SLOPE)
        seg_max = jax.ops.segment_max(b, dst, num_segments=n)
        ex = jnp.exp(b - seg_max[dst])
        denom = jax.ops.segment_sum(ex, dst, num_segments=n)
        alpha = ex / denom[dst]
        out = jax.ops.segment_sum(c * alpha[:, None], dst, num_segments=n)
        return jax.nn.leaky_relu(out, SLOPE)

    def _L1_gnn_ref(feats, src, dst):
        import jax, jax.numpy as jnp
        import numpy as np
        N_NODES = 100000
        N_EDGES = 25000
        D_FEAT = 128
        n_nodes = feats.shape[0]
        msgs = feats[src]
        agg = jax.ops.segment_sum(msgs, dst, num_segments=n_nodes)
        deg = jax.ops.segment_sum(jnp.ones_like(dst, dtype=feats.dtype), dst, num_segments=n_nodes)
        out = jnp.where((deg > 0)[:, None], agg, feats)
        return out
    edge_index = jnp.stack([src, dst])
    h = jnp.maximum(_layernorm(x, axis=-1), 0.0)
    x = x + _L0_gnn_ref(h, L0_gnn_relation_embedding, L0_gnn_W1, L0_gnn_b1, L0_gnn_w2, edge_index, edge_type_200)
    h = jnp.maximum(_layernorm(x, axis=-1), 0.0)
    x = x + _L1_gnn_ref(h, src, dst)
    return x

_drawn_inputs = setup_inputs


def setup_inputs(seed=0):
    import zlib

    import numpy as np

    out = dict(_drawn_inputs(seed))
    spreads = {'L0_gnn_b1': (0.0, 0.1)}
    factors = {'L0_gnn_w2': 6.054}
    for name, (base, spread) in spreads.items():
        noise = np.random.default_rng([zlib.crc32(name.encode()), seed]).standard_normal(out[name].shape)
        drawn = base * np.exp(spread * noise) if base else spread * noise
        out[name] = jnp.asarray(drawn.astype(out[name].dtype))
    for name, factor in factors.items():
        out[name] = (out[name] * factor).astype(out[name].dtype)
    return out
```

```python
import concourse.bass as bass
from concourse import mybir
from contextlib import ExitStack

P = 128
D = 128
GS = 16
BG = 4
NBLK = GS // BG
EPS = 1e-5
SLOPE = 0.01
FAR = float(2.0 ** 100)
SKIP = float(2 ** 20)
OFF = 200.0


def wait(engine, semaphore, value):
    if isinstance(value, int) and value <= 0:
        return
    engine.wait_ge(semaphore, value)


class At:

    def __init__(self, i, k):
        self.n = 4 * i + k
        self.slot4, self.round4 = k % 4, i + k // 4
        self.slot2, self.round2 = k % 2, 2 * i + k // 2


class Steps:

    def __init__(self, engine, semaphore, done):
        self.engine, self.semaphore, self.done = engine, semaphore, done
        self.n = 0

    def mark(self, instruction):
        self.n += 1
        instruction.then_inc(self.semaphore, 1)

    def settle(self):
        self.engine.wait_ge(self.semaphore, self.done + self.n)

    def then(self, instruction):
        self.mark(instruction)
        self.settle()


class Semaphores:

    def __init__(self, sem, n):
        self.x_in = [sem(f"x_in{s}_{n}") for s in range(4)]
        self.idx_in = [sem(f"idx_in{s}_{n}") for s in range(4)]
        self.rows_in = [sem(f"rows_in{s}_{n}") for s in range(2)]
        self.gathered = [sem(f"gathered{s}_{n}") for s in range(2)]
        self.stored = [sem(f"stored{s}_{n}") for s in range(4)]
        self.var = sem(f"var_{n}")
        self.rstd0 = sem(f"rstd0_{n}")
        self.rstd = sem(f"rstd_{n}")
        self.ae = sem(f"ae_{n}")
        self.an = sem(f"an_{n}")
        self.sel = sem(f"sel_{n}")
        self.y = sem(f"y_{n}")
        self.yfree = sem(f"yfree_{n}")
        self.x1 = sem(f"x1_{n}")
        self.act = sem(f"act_{n}")
        self.first = sem(f"first_{n}")
        self.second = sem(f"second_{n}")
        self.turns = sem(f"turns_{n}")
        self.row_turns = sem(f"row_turns_{n}")
        self.rest_in = sem(f"rest_in_{n}")
        if n == 2:
            return
        self.tn = sem("tn")
        self.te = sem("te")
        self.hn = sem("hn")
        self.he = sem("he")
        self.oh = sem("oh")
        self.c = sem("c")
        self.cs = sem("cs")
        self.sn = sem("sn")
        self.sn3 = sem("sn3")
        self.sd = sem("sd")
        self.b = sem("b")
        self.bT = sem("bT")
        self.d = sem("d")
        self.w = sem("w")
        self.al = sem("al")
        self.alT = sem("alT")
        self.qc = sem("qc")
        self.split = sem("split")
        self.hasr = sem("hasr")


def gnn_two_layers(nc, x, src_e, dst_e, typ_e, rel, w1, b1, w2, out):
    f32, bf16, i32, u32 = mybir.dt.float32, mybir.dt.bfloat16, mybir.dt.int32, mybir.dt.uint32
    ALU, ACT, AX = mybir.AluOpType, mybir.ActivationFunctionType, mybir.AxisListType.X

    N = x.shape[0]
    EC = dst_e.shape[1] // P
    R = rel.shape[0]
    RB = R - P
    NSB = -(-N // (GS * P))
    NG = NSB * GS
    NK = -(-NG // P)
    LOOPS = (NSB - 1) // 4
    assert NSB == 4 * LOOPS + 1 and EC % 4 == 0
    TAIL = N - (NSB - 1) * GS * P
    TG, TR = TAIL // P, TAIL % P
    assert TG > 1

    starts_d = nc.dram_tensor("starts_d", (1024, 1), i32, kind="Internal").ap()
    scan_d = nc.dram_tensor("scan_d", (NK * P, 4 * P), f32, kind="Internal").ap()
    place_d = nc.dram_tensor("place_d", (NK * P, P), bf16, kind="Internal").ap()
    types_d = nc.dram_tensor("types_d", (NK * P, P), bf16, kind="Internal").ap()
    x1_d = nc.dram_tensor("x1_d", (N, D), f32, kind="Internal").ap()

    ctx = ExitStack()
    with ctx:
        def sb(name, shape, dt):
            return ctx.enter_context(nc.sbuf_tensor(name, shape, dt))

        def pb(name, shape, dt):
            return ctx.enter_context(nc.psum_tensor(name, shape, dt))

        def sem(name):
            return ctx.enter_context(nc.semaphore(name))

        ident = sb("ident", [P, P], f32)
        row = sb("row", [P, P], f32)
        col = sb("col", [P, 2], f32)
        gbase = sb("gbase", [P, NK], f32)
        fold = sb("fold", [P, 32], f32)
        below = sb("below", [32, 32], f32)
        blocks4 = sb("blocks4", [P, 4], f32)
        row32 = sb("row32", [P, 32], f32)
        ones = sb("ones", [P, 1], f32)
        w1s = sb("w1s", [P, 3, D], f32)
        w2b = sb("w2b", [P, D], f32)
        b1b = sb("b1b", [P, D], f32)
        rels = sb("rels", [P, 2, D], f32)
        relT = sb("relT", [P, 2 * P], f32)
        w1a = sb("w1a", [P, D + 1], f32)
        ub = sb("ub", [P, 1], f32)
        relw = sb("relw", [P, 2, D + 1], f32)
        rel3 = sb("rel3", [P, 2, 3, D + 1], bf16)
        junk = sb("junk", [P, D + 1], f32)

        idx_t = sb("idx_t", [P, NK * P], u32)
        plc_t = sb("plc_t", [P, NK * P], f32)
        has_t = sb("has_t", [P, NG], f32)

        xn = sb("xn", [P, 4, GS, D], f32)
        xe = sb("xe", [P, 2, GS, D], f32)
        an = sb("an", [P, 2, BG, D], f32)
        ae = sb("ae", [P, 2, BG, D], f32)
        heT = sb("heT", [P, 2, BG * P], f32)
        hnT = sb("hnT", [P, 2, GS * P], f32)
        cs = sb("cs", [P, 2, GS, D + 1], f32)
        sel = sb("sel", [P, 2, BG, P], f32)
        plr = sb("plr", [P, 2, GS * P], bf16)
        tyr = sb("tyr", [P, 2, GS * P], bf16)
        ota = sb("ota", [P, 2, GS * P], bf16)
        otb = sb("otb", [P, 2, GS * P], bf16)
        selT = sb("selT", [P, 2, GS * P], bf16)
        scn = sb("scn", [GS, 2, 4, P], f32)
        plc = sb("plc", [P, 2, GS], f32)
        idx = sb("idx", [P, 4, GS], u32)
        qc = sb("qc", [P, 2, BG * D], f32)
        lr = sb("lr", [P, 2, BG * D], f32)
        st = sb("st", [P, 2 * GS, 6], f32)
        tiny = sb("tiny", [P, 12, 2 * GS], f32)
        rstd0 = sb("rstd0", [P, 2 * GS], f32)
        lnv = sb("lnv", [P, 2 * GS], f32)
        var = sb("var", [P, 2 * GS], f32)
        rstd = sb("rstd", [P, 2 * GS], f32)
        nbias = sb("nbias", [P, 2 * GS], f32)
        sn3 = sb("sn3", [P, GS, 3], bf16)
        snr = sb("snr", [P, 2, GS], f32)
        sc = sb("sc", [P, 3, GS], f32)
        rows = sb("rows", [P, 8, P], f32)
        alpha = sb("alpha", [P, 2, GS], f32)
        has = sb("has", [P, GS], f32)

        tn_p = pb("tn_p", [P, BG * P], f32)
        te_p = pb("te_p", [P, 2, BG * P], f32)
        c_p = pb("c_p", [P, 2, 512], f32)
        y_p = pb("y_p", [P, 2, BG * D], f32)
        s_p = pb("s_p", [P, 512], f32)
        sn_p, sd_p = s_p[:, 0:GS], s_p[:, GS:4 * GS]
        bT_p, alT_p = s_p[0:GS, 64:64 + P], s_p[:, 192:192 + GS]
        has_p = s_p[:, 256:256 + 16 * NBLK].rearrange("p (q c) -> p q c", c=16)

        k_in = sem("k_in")
        k_const = sem("k_const")
        k_pool = sem("k_pool")
        k_dve = sem("k_dve")
        k_pe = sem("k_pe")
        k_start = sem("k_start")
        k_startl = sem("k_startl")
        k_gat = [sem(f"k_gat{i}") for i in range(2)]
        k_free = sem("k_free")
        k_idx = sem("k_idx")
        k_tr = sem("k_tr")
        k_out = [sem(f"k_out{i}") for i in range(2)]
        k_rows = sem("k_rows")

        with ExitStack() as ctx1:
            dsti = xn[:, 0, 0:4, :].rearrange("p a b -> p (a b)")[:, 0:EC].bitcast(i32)
            hi_i = xn[:, 0, 4:8, :].rearrange("p a b -> p (a b)")[:, 0:EC].bitcast(i32)
            lo_i = xn[:, 0, 8:12, :].rearrange("p a b -> p (a b)")[:, 0:EC].bitcast(i32)
            hi_f = xn[:, 1, 0:4, :].rearrange("p a b -> p (a b)")[:, 0:EC]
            lo_f = xn[:, 1, 4:8, :].rearrange("p a b -> p (a b)")[:, 0:EC]
            CH = EC // 4
            oh_h = hnT[:, :, :].rearrange("p a b -> p (a b)").bitcast(bf16)[:, 0:CH * 32].rearrange("p (c h) -> p c h", h=32)
            oh_l = cs[:, 0, :, :].rearrange("p a b -> p (a b)").bitcast(bf16)[:, 0:CH * 32].rearrange("p (c h) -> p c h", h=32)
            hist_p = tn_p[:, 0:P]
            cnt_p = tn_p[0:32, 128:160]
            pre_p = tn_p[0:32, 160:161]
            histm = sel[:, 0, 0, :]
            histr = sel[:, 0, 1, 0:32]
            cnt = sel[0:32, 0, 2, 0:32]
            cum = sel[0:32, 0, 2, 32:64]
            pre = sel[0:32, 0, 2, 64:65]
            zero32 = sel[0:32, 0, 2, 96:128]
            sta = sel[0:32, 0, 3, 0:32]
            stai = sel[0:32, 0, 3, 32:64].bitcast(i32)
            first = lr[:, 0, 0:NK].bitcast(i32)
            gd = [xe[:, i, 0, :].bitcast(i32) for i in range(2)]
            gs_ = [xe[:, i, 1, :].bitcast(i32) for i in range(2)]
            gt = [xe[:, i, 2, :].bitcast(i32) for i in range(2)]
            plf = [xe[:, i, 3, :] for i in range(2)]
            idf = [xe[:, i, 4, :] for i in range(2)]
            srf = [xe[:, i, 5, :] for i in range(2)]
            mf = [xe[:, i, 6:10, :] for i in range(2)]
            plb = [xe[:, i, 10, 0:64].bitcast(bf16) for i in range(2)]
            tyb = [xe[:, i, 11, 0:64].bitcast(bf16) for i in range(2)]

            block = ctx1.enter_context(nc.Block())
            NIN = 6

            @block.sync
            def _(sp):
                sp.dma_start(dsti, dst_e.rearrange("o (p c) -> (o p) c", p=P)).then_inc(k_in, 16)
                sp.dma_start(w1s[:, :, :], w1.rearrange("(a p) d -> p a d", p=P)).then_inc(k_in, 16)
                sp.dma_start(rels[:, 0, :], rel[0:P, :]).then_inc(k_in, 16)
                sp.dma_start(rels[0:RB, 1, :], rel[P:R, :]).then_inc(k_in, 16)
                sp.dma_start(w2b[:, :], w2.partition_broadcast(P)).then_inc(k_in, 16)
                sp.dma_start(b1b[:, :], b1.partition_broadcast(P)).then_inc(k_in, 16)
                sp.wait_ge(k_start, 1)
                sp.dma_start(starts_d.rearrange("(h l) o -> h (l o)", l=32), stai).then_inc(k_startl, 16)
                sp.wait_ge(k_startl, 16)
                sp.dma_start(first, starts_d[0:NK * P, :].rearrange("(k p) o -> p (k o)", p=P),
                             allow_slow_non_contiguous=True).then_inc(k_startl, 16)
                for k in range(NK):
                    sp.wait_ge(k_rows, k + 1)
                    for table, made in ((scan_d, mf[k % 2].rearrange("p a b -> p (a b)")), (place_d, plb[k % 2]), (types_d, tyb[k % 2])):
                        sp.dma_start(table[k * P:(k + 1) * P, :], made).then_inc(k_out[k % 2], 16)
                for i in range(2):
                    sp.wait_ge(k_out[i], 48 * ((NK + 1 - i) // 2))

            @block.gpsimd
            def _(pool):
                g = nc.gpsimd
                steps = Steps(pool, k_pool, 0)
                g.iota(row[:, :], pattern=[[1, P]], base=0, channel_multiplier=0, allow_small_or_imprecise_dtypes=True)
                g.iota(row32[:, :], pattern=[[1, 32]], base=0, channel_multiplier=0, allow_small_or_imprecise_dtypes=True)
                g.iota(col[:, :], pattern=[[P, 2]], base=0, channel_multiplier=1, allow_small_or_imprecise_dtypes=True)
                g.iota(gbase[:, :], pattern=[[P * P, NK]], base=0, channel_multiplier=P, allow_small_or_imprecise_dtypes=True)
                g.memset(ident[:, :], 0.0)
                g.memset(ones[:, :], 1.0)
                g.memset(fold[:, :], 0.0)
                g.memset(below[:, :], 1.0)
                steps.then(g.memset(blocks4[:, :], 1.0))
                g.affine_select(out=ident[:, :], in_=ident[:, :], compare_op=ALU.not_equal, fill=1.0, base=0,
                                pattern=[[-1, P]], channel_multiplier=1)
                g.affine_select(out=below[:, :], in_=below[:, :], compare_op=ALU.is_gt, fill=0.0, base=0,
                                pattern=[[1, 32]], channel_multiplier=-1)
                steps.then(g.affine_select(out=blocks4[:, :], in_=blocks4[:, :], compare_op=ALU.is_ge, fill=0.0, base=0,
                                           pattern=[[-32, 4]], channel_multiplier=1))
                steps.then(g.affine_select(out=blocks4[:, :], in_=blocks4[:, :], compare_op=ALU.is_ge, fill=0.0, base=31,
                                           pattern=[[32, 4]], channel_multiplier=-1))
                for a in range(4):
                    steps.then(g.affine_select(out=fold[:, :], in_=fold[:, :], compare_op=ALU.not_equal, fill=1.0,
                                               base=-32 * a, pattern=[[-1, 32]], channel_multiplier=1))
                g.memset(zero32, 0.0).then_inc(k_const, 1)
                pool.wait_ge(k_startl, 32)
                for k in range(NK):
                    wait(pool, k_free, k - 1)
                    for to, e in ((gs_, src_e), (gd, dst_e), (gt, typ_e)):
                        g.indirect_dma_start(out=to[k % 2], out_offset=None, in_=e,
                                             in_offset=bass.IndirectOffsetOnAxis(ap=first[:, k:k + 1].bitcast(u32), axis=1)
                                             ).then_inc(k_gat[k % 2], 16)

            @block.tensor
            def _(pe):
                pe.wait_ge(k_const, 1)
                pe.wait_ge(k_in, 16 * NIN)
                nc.tensor.transpose(te_p[:, 0, 0:P], rels[:, 0, :], ident[:, :])
                nc.tensor.transpose(te_p[:, 0, P:P + RB], rels[0:RB, 1, :], ident[0:RB, 0:RB]).then_inc(k_pe, 1)
                for c in range(4):
                    pe.wait_ge(k_idx, c + 1)
                    for j in range(CH // 4 + (CH % 4 > 0)):
                        w = min(4, CH - 4 * j)
                        last = nc.tensor.matmul(hist_p[0:32 * w, 0:32 * w],
                                                oh_h[:, 4 * j:4 * j + w, :].rearrange("p c h -> p (c h)"),
                                                oh_l[:, 4 * j:4 * j + w, :].rearrange("p c h -> p (c h)"),
                                                start=(c == 0 and j == 0), stop=(c == 3 and 4 * j + w == CH),
                                                skip_group_check=True)
                    last.then_inc(k_tr, 1)
                pe.wait_ge(k_idx, 5)
                nc.tensor.matmul(cnt_p, fold[:, :], histr, start=True, stop=True).then_inc(k_tr, 1)
                pe.wait_ge(k_idx, 6)
                nc.tensor.matmul(pre_p, below[:, :], cum[:, 31:32], start=True, stop=True).then_inc(k_tr, 1)
                pe.wait_ge(k_idx, 7)
                nc.tensor.matmul(te_p[:, 1, 0:P], relT[:, 0:P], w1s[:, 2, :], start=True, stop=True)
                nc.tensor.matmul(te_p[0:RB, 1, P:2 * P], relT[:, P:P + RB], w1s[:, 2, :], start=True, stop=True).then_inc(k_tr, 1)
                for k in range(NK):
                    pe.wait_ge(k_rows, k + 1)
                    wait(pe, k_free, k - 1)
                    nc.tensor.transpose(c_p[:, k % 2, 0:P], idf[k % 2], ident[:, :])
                    nc.tensor.transpose(c_p[:, k % 2, P:2 * P], plf[k % 2], ident[:, :]).then_inc(k_pe, 1)

            @block.vector
            def _(dve):
                v = nc.vector
                steps = Steps(dve, k_dve, 0)
                dve.wait_ge(k_in, 16 * NIN)
                dve.wait_ge(k_const, 1)
                v.tensor_scalar(hi_i, dsti, 12, None, ALU.logical_shift_right)
                steps.then(v.tensor_scalar(lo_i, dsti, 20, 27, ALU.logical_shift_left, ALU.logical_shift_right))
                v.tensor_copy(hi_f, hi_i)
                steps.then(v.tensor_copy(lo_f, lo_i))
                for c in range(4):
                    wait(dve, k_tr, c)
                    r32 = row32[:, :].unsqueeze(1).to_broadcast([P, CH, 32])
                    v.tensor_tensor(oh_h, hi_f[:, c * CH:(c + 1) * CH].unsqueeze(2).to_broadcast([P, CH, 32]), r32, ALU.is_equal)
                    v.tensor_tensor(oh_l, lo_f[:, c * CH:(c + 1) * CH].unsqueeze(2).to_broadcast([P, CH, 32]), r32,
                                    ALU.is_equal).then_inc(k_idx, 1)
                dve.wait_ge(k_tr, 4)
                steps.then(v.tensor_tensor(histm.rearrange("p (a l) -> p a l", a=4), hist_p.rearrange("p (a l) -> p a l", a=4),
                                           blocks4[:, :].unsqueeze(2).to_broadcast([P, 4, 32]), ALU.mult))
                v.tensor_reduce(histr, histm.rearrange("p (a l) -> p l a", a=4), AX, ALU.add).then_inc(k_idx, 1)
                dve.wait_ge(k_tr, 5)
                steps.then(v.tensor_copy(cnt, cnt_p))
                v.tensor_tensor_scan(cum, zero32, cnt, 0.0, ALU.add, ALU.add).then_inc(k_idx, 1)
                dve.wait_ge(k_idx, 6)
                dve.wait_ge(k_tr, 6)
                steps.then(v.tensor_copy(pre, pre_p))
                steps.then(v.scalar_tensor_tensor(sta, cum, pre, cnt, ALU.add, ALU.subtract))
                v.tensor_copy(stai, sta).then_inc(k_start, 1)
                dve.wait_ge(k_pe, 1)
                v.tensor_copy(relT[:, 0:P + RB], te_p[:, 0, 0:P + RB]).then_inc(k_idx, 1)
                v.tensor_copy(w1a[:, 0:D], w1s[:, 0, :])

                def dot_w2(into, a, n):
                    steps.then(v.tensor_tensor_reduce(out=junk[0:n, 0:D], in0=a, in1=w2b[0:n, :], scale=1.0, scalar=0.0,
                                                      op0=ALU.mult, op1=ALU.add, accum_out=into))

                dot_w2(w1a[:, D:D + 1], w1s[:, 0, :], P)
                dot_w2(ub[:, :], w1s[:, 1, :], P)
                dve.wait_ge(k_tr, 7)
                for c, n in ((0, P), (1, RB)):
                    steps.then(v.tensor_tensor(relw[0:n, c, 0:D], te_p[0:n, 1, c * P:c * P + D], b1b[0:n, :], ALU.add))
                    dot_w2(relw[0:n, c, D:D + 1], relw[0:n, c, 0:D], n)
                    steps.then(v.tensor_copy(rel3[0:n, c, 0, :], relw[0:n, c, :]))
                    steps.then(v.tensor_tensor(junk[0:n, :], relw[0:n, c, :], rel3[0:n, c, 0, :], ALU.subtract))
                    steps.then(v.tensor_copy(rel3[0:n, c, 1, :], junk[0:n, :]))
                    steps.then(v.tensor_tensor(rel3[0:n, c, 2, :], junk[0:n, :], rel3[0:n, c, 1, :], ALU.subtract))
                for k in range(NK):
                    i = k % 2
                    dve.wait_ge(k_gat[i], 48 * (k // 2 + 1))
                    wait(dve, k_out[i], 48 * (k // 2))
                    p, m = plf[i], mf[i]
                    v.tensor_copy(srf[i], gs_[i])
                    v.tensor_copy(tyb[i], gt[i])
                    steps.then(v.tensor_copy(p, gd[i]))
                    steps.then(v.tensor_scalar(p, p, gbase[:, k:k + 1], OFF, ALU.subtract, ALU.min))
                    v.tensor_copy(plb[i], p)
                    v.tensor_scalar(idf[i], p, float(P - 1), SKIP, ALU.is_gt, ALU.mult)
                    v.memset(m[:, 2, 0:1], 0.0)
                    v.memset(m[:, 3, P - 1:P], 0.0)
                    v.tensor_tensor(m[:, 2, 1:P], p[:, 1:P], p[:, 0:P - 1], ALU.is_equal)
                    steps.then(v.tensor_tensor(m[:, 3, 0:P - 1], p[:, 0:P - 1], p[:, 1:P], ALU.is_equal))
                    v.tensor_scalar(m[:, 0:2, :], m[:, 2:4, :], 1.0, FAR, ALU.subtract, ALU.mult)
                    v.tensor_tensor(idf[i], idf[i], srf[i], ALU.add).then_inc(k_rows, 1)
                    dve.wait_ge(k_pe, k + 2)
                    v.tensor_copy(idx_t[:, k * P:(k + 1) * P], c_p[:, i, 0:P])
                    v.tensor_copy(plc_t[:, k * P:(k + 1) * P], c_p[:, i, P:2 * P]).then_inc(k_free, 1)
                dve.wait_ge(k_free, NK)
                for i in range(2):
                    dve.wait_ge(k_out[i], 48 * ((NK + 1 - i) // 2))
                v.memset(xe[:, :, :, :], 0.0)
                v.memset(rows[:, :, :], 0.0)
                for i in range(4):
                    last = v.memset(xn[:, i, :, :], 0.0)
                last.then_inc(k_free, 1)

        L1, L2 = Semaphores(sem, 1), Semaphores(sem, 2)

        block = ctx.enter_context(nc.Block())

        def nodes_of(a, t, tail):
            if not tail:
                half = GS // 2
                return [(a[bass.ds(t.n * GS * P + h * half * P, half * P), :].rearrange("(g p) d -> p g d", p=P),
                         h * half, (h + 1) * half, P) for h in range(2)]
            at = (NSB - 1) * GS * P
            parts = []
            if TG:
                half = TG // 2
                for g0, g1 in ((0, half), (half, TG)):
                    parts.append((a[at + g0 * P:at + g1 * P, :].rearrange("(g p) d -> p g d", p=P), g0, g1, P))
            if TR:
                parts.append((a[at + TG * P:N, :].rearrange("(g p) d -> p g d", p=TR), TG, TG + 1, TR))
            return parts

        NTAIL = 2 + (TR > 0)

        @block.sync
        def _(sp):
            def done(L, n):
                if L is L1:
                    wait(sp, L1.x1, n)
                elif not (isinstance(n, int) and n <= 0):
                    sp.wait_ge(L2.yfree, 2 + NBLK * n)

            def load_x(L, a, t, tail=False):
                wait(sp, L.stored[t.slot4], 32 * t.round4)
                first, second, *rest = nodes_of(a, t, tail)
                for r_rows, r0, r1, r_np in rest:
                    sp.dma_start(xn[0:r_np, t.slot4, r0:r1, :], r_rows).then_inc(L.rest_in, 16)
                    sp.wait_ge(L.rest_in, 16)
                for rows_, g0, g1, np_ in (first, second):
                    sp.dma_start(xn[0:np_, t.slot4, g0:g1, :], rows_).then_inc(L.x_in[t.slot4], 16)

            def load_idx(L, t):
                wait(sp, L.gathered[t.slot2], 256 * (t.round2 - 1))
                sp.dma_start(idx[:, t.slot4, :], idx_t[:, bass.ds(t.n * GS, GS)]).then_inc(L.idx_in[t.slot4], 16)

            def load_rows(L, n, t):
                done(L, t.n - 1)
                sp.sem_inc(L.row_turns, 1)
                sp.dma_start(plc[:, t.slot2, :], plc_t[:, bass.ds(t.n * GS, GS)]).then_inc(L.rows_in[t.slot2], 16)
                if n == 1:
                    sp.dma_start(scn[:, t.slot2, :, :].rearrange("g a b -> g (a b)"),
                                 scan_d[bass.ds(t.n * GS, GS), :]).then_inc(L.rows_in[t.slot2], 16)
                    for to, table in ((plr, place_d), (tyr, types_d)):
                        sp.dma_start(to[:, t.slot2, :],
                                     table[bass.ds(t.n * GS, GS), :].rearrange("g s -> (g s)").partition_broadcast(P)
                                     ).then_inc(L.rows_in[t.slot2], 16)

            def store(L, a, t, tail=False):
                done(L, t.n + 1)
                for rows_, g0, g1, np_ in nodes_of(a, t, tail):
                    sp.dma_start(rows_, xn[0:np_, t.slot4, g0:g1, :]).then_inc(L.stored[t.slot4], 16)

            def layer(L, n, a, to):
                for k in range(3):
                    load_x(L, a, At(0, k))
                    load_idx(L, At(0, k))
                for k in range(2):
                    load_rows(L, n, At(0, k))

                def turn(i, k, last=False):
                    store(L, to, At(i, k))
                    if not last or k < 2:
                        load_x(L, a, At(i, k + 3), tail=last and k == 1)
                        load_idx(L, At(i, k + 3))
                    if not last or k < 3:
                        load_rows(L, n, At(i, k + 2))

                for k in range(4):
                    turn(0, k)
                with nc.sync.Fori(1, LOOPS - 1) as i:
                    for k in range(4):
                        turn(i, k)
                for k in range(4):
                    turn(LOOPS - 1, k, last=True)
                store(L, to, At(LOOPS, 0), tail=True)
                for s in range(4):
                    sp.wait_ge(L.stored[s], 32 * LOOPS + (16 * NTAIL if s == 0 else 0))

            sp.wait_ge(k_free, NK + 1)
            layer(L1, 1, x, x1_d)
            layer(L2, 2, x1_d, out)

        @block.gpsimd
        def _(pool):
            def gather(L, a, t):
                wait(pool, L.idx_in[t.slot4], 16 * (t.round4 + 1))
                wait(pool, L.ae, NBLK * (t.n - 1))
                pool.sem_inc(L.turns, 1)
                for j in range(GS):
                    nc.gpsimd.indirect_dma_start(out=xe[:, t.slot2, j, :], out_offset=None, in_=a,
                                                 in_offset=bass.IndirectOffsetOnAxis(ap=idx[:, t.slot4, j:j + 1], axis=0),
                                                 bounds_check=last_row, oob_is_err=False).then_inc(L.gathered[t.slot2], 16)

            pool.wait_ge(k_free, NK + 1)
            last_row = nc.gpsimd.to_reg(N - 1)
            for L, a in ((L1, x), (L2, x1_d)):
                if L is L2:
                    for s in range(4):
                        pool.wait_ge(L1.stored[s], 32 * LOOPS + (16 * NTAIL if s == 0 else 0))
                for k in range(5):
                    gather(L, a, At(0, k))
                with nc.gpsimd.Fori(1, LOOPS) as i:
                    for k in range(1, 5):
                        gather(L, a, At(i, k))

        h2 = hnT[:, :, :].rearrange("p s (g d) -> p s g d", g=GS)
        own = cs[:, :, :, 0:D]

        def run(engine_fori, first, second):
            first(At(0, 0), None)
            for k in range(1, 5):
                first(At(0, k), At(0, k - 1))
            with engine_fori(1, LOOPS) as i:
                for k in range(1, 5):
                    first(At(i, k), At(i, k - 1))
            second(At(LOOPS, 0))

        @block.vector
        def _(dve):
            v = nc.vector

            def stats(L, n, t, k_first):
                steps = Steps(dve, L.first, k_first * t.n)
                dve.wait_ge(L.x_in[t.slot4], 32 * (t.round4 + 1))
                for j in range(GS):
                    v.bn_stats(st[:, GS + j, :], xn[:, t.slot4, j, :])
                dve.wait_ge(L.gathered[t.slot2], 256 * (t.round2 + 1))
                for j in range(GS):
                    last = v.bn_stats(st[:, j, :], xe[:, t.slot2, j, :])
                steps.then(last)
                msum, dm, m2, dm2, m2e = (tiny[:, c, :] for c in range(5))
                v.tensor_tensor(msum, st[:, :, 1], st[:, :, 4], ALU.add)
                v.tensor_tensor(dm, st[:, :, 1], st[:, :, 4], ALU.subtract)
                steps.then(v.tensor_tensor(m2, st[:, :, 2], st[:, :, 5], ALU.add))
                v.scalar_tensor_tensor(dm2, dm, 0.25, dm, ALU.mult, ALU.mult)
                steps.then(v.tensor_scalar(m2e, m2, 1.0 / D, EPS, ALU.mult, ALU.add))
                v.tensor_tensor(var[:, :], dm2, m2e, ALU.add).then_inc(L.var, 1)
                dve.wait_ge(L.rstd0, t.n + 1)
                t0, t1 = tiny[:, 5, :], tiny[:, 6, :]
                steps.then(v.tensor_tensor(t0, var[:, :], rstd0[:, :], ALU.mult))
                steps.then(v.scalar_tensor_tensor(t1, t0, -0.5, rstd0[:, :], ALU.mult, ALU.mult))
                wait(dve, L.ae, NBLK * t.n)
                if n == 2:
                    wait(dve, L.an, NBLK * t.n)
                    v.tensor_scalar(tiny[:, 7, 0:GS], has_t[:, bass.ds(t.n * GS, GS)], -1.0, 1.0, ALU.mult, ALU.add)
                steps.then(v.scalar_tensor_tensor(rstd[:, :], t1, 1.5, rstd0[:, :], ALU.add, ALU.mult))
                if n == 2:
                    steps.then(v.tensor_tensor(rstd[:, GS:2 * GS], rstd[:, GS:2 * GS], tiny[:, 7, 0:GS], ALU.mult))
                v.scalar_tensor_tensor(nbias[:, :], msum, -0.5, rstd[:, :], ALU.mult, ALU.mult).then_inc(L.rstd, 1)
                assert steps.n == k_first, steps.n

            def first1(t, m):
                L = L1
                stats(L, 1, t, 6)
                dve.wait_ge(L.rstd, t.n + 1)
                for q in range(NBLK):
                    wait(dve, L.tn, NBLK * t.n + q - 1)
                    for j in range(BG):
                        g = q * BG + j
                        last = v.tensor_scalar(an[:, q % 2, j, :], xn[:, t.slot4, g, :], rstd[:, GS + g:GS + g + 1],
                                               nbias[:, GS + g:GS + g + 1], ALU.mult, ALU.add)
                    last.then_inc(L.an, 1)
                dve.wait_ge(L.rows_in[t.slot2], 64 * (t.round2 + 1))
                wait(dve, L.sd, t.n - 1)
                v.tensor_scalar(ota[:, t.slot2, :], tyr[:, t.slot2, :], col[:, 0:1], None, ALU.is_equal)
                v.tensor_scalar(otb[:, t.slot2, :], tyr[:, t.slot2, :], col[:, 1:2], None, ALU.is_equal)
                v.tensor_scalar(selT[:, t.slot2, :], plr[:, t.slot2, :], col[:, 0:1], None, ALU.is_equal).then_inc(L.oh, 1)
                if m is not None:
                    second1(m)
                steps = Steps(dve, L.split, 3 * t.n)
                dve.wait_ge(L.sn, t.n + 1)
                steps.then(v.tensor_copy(sn3[:, :, 0], sn_p))
                steps.then(v.tensor_tensor(snr[:, 0, :], sn_p, sn3[:, :, 0], ALU.subtract))
                steps.then(v.tensor_copy(sn3[:, :, 1], snr[:, 0, :]))
                v.tensor_tensor(sn3[:, :, 2], snr[:, 0, :], sn3[:, :, 1], ALU.subtract).then_inc(L.sn3, 1)

            SOFT = 8
            K_SECOND = SOFT + NBLK

            def second1(m):
                L = L1
                steps = Steps(dve, L.second, K_SECOND * m.n)
                sd, b0, b = sc[:, 0, :], sc[:, 1, :], sc[:, 2, :]
                dve.wait_ge(L.sd, m.n + 1)
                dve.wait_ge(L.cs, NBLK * (m.n + 1))
                steps.then(v.tensor_reduce(sd, sd_p.rearrange("p (g a) -> p g a", a=3), AX, ALU.add))
                steps.then(v.tensor_tensor(b0, sd, cs[:, m.slot2, :, D], ALU.add))
                v.scalar_tensor_tensor(b, b0, SLOPE, b0, ALU.mult, ALU.max).then_inc(L.b, 1)
                dve.wait_ge(L.bT, m.n + 1)
                mF, mB, d, w, sF, sB, rc, al = (rows[0:GS, c, :] for c in range(8))
                reset = scn[:, m.slot2, :, :]
                steps.then(v.tensor_tensor_scan(mF, reset[:, 0, :], bT_p, -FAR, ALU.add, ALU.max))
                steps.then(v.tensor_tensor_scan(mB[:, ::-1], reset[:, 1, ::-1], mF[:, ::-1], -FAR, ALU.add, ALU.max))
                v.tensor_tensor(d, bT_p, mB, ALU.subtract).then_inc(L.d, 1)
                dve.wait_ge(L.w, m.n + 1)
                steps.then(v.tensor_tensor_scan(sF, reset[:, 2, :], w, 0.0, ALU.mult, ALU.add))
                steps.then(v.tensor_tensor_scan(sB[:, ::-1], reset[:, 3, ::-1], sF[:, ::-1], 0.0, ALU.mult, ALU.max))
                steps.then(v.reciprocal(rc, sB))
                v.tensor_tensor(al, w, rc, ALU.mult).then_inc(L.al, 1)
                dve.wait_ge(L.alT, m.n + 1)
                steps.then(v.tensor_copy(alpha[:, 0, :], alT_p))
                for q in range(NBLK + 1):
                    if q < NBLK:
                        if q >= 2:
                            dve.wait_ge(L.y, NBLK * m.n + q - 1)
                        for j in range(BG):
                            g = q * BG + j
                            last = v.tensor_scalar(sel[:, q % 2, j, :], row[:, :], plc[:, m.slot2, g:g + 1],
                                                   alpha[:, 0, g:g + 1], ALU.is_equal, ALU.mult)
                        last.then_inc(L.sel, 1)
                    if q > 0:
                        f, g0 = q - 1, (q - 1) * BG
                        dve.wait_ge(L.y, NBLK * m.n + f + 1)
                        v.tensor_scalar(has[:, g0:g0 + BG], has_p[:, f, 0:BG], 0.5, None, ALU.is_gt).then_inc(L.hasr, 1)
                        dve.wait_ge(L.qc, NBLK * m.n + f + 1)
                        if f >= 2:
                            dve.wait_ge(L.second, steps.done + SOFT + f - 1)
                        v.tensor_tensor(lr[:, f % 2, :], y_p[:, f % 2, :], qc[:, f % 2, :], ALU.max).then_inc(L.yfree, 1)
                        dve.wait_ge(L.yfree, 2 + NBLK * m.n + f + 1)
                        for j in range(BG):
                            xs = xn[:, m.slot4, g0 + j, :]
                            last = v.scalar_tensor_tensor(xs, lr[:, f % 2, j * D:(j + 1) * D], has[:, g0 + j:g0 + j + 1], xs,
                                                          ALU.mult, ALU.add)
                        if f < NBLK - 1:
                            steps.mark(last)
                last.then_inc(L.x1, 1)
                steps.mark(v.tensor_copy(has_t[:, bass.ds(m.n * GS, GS)], has[:, :]))
                assert steps.n == K_SECOND, steps.n

            def first2(t, m):
                stats(L2, 2, t, 7)
                if m is not None:
                    second2(m)

            def second2(m):
                L = L2
                dve.wait_ge(L.rows_in[m.slot2], 16 * (m.round2 + 1))
                for q in range(NBLK + 1):
                    if q < NBLK:
                        if q >= 2:
                            dve.wait_ge(L.y, NBLK * m.n + q - 1)
                        for j in range(BG):
                            g = q * BG + j
                            last = v.tensor_scalar(sel[:, q % 2, j, :], row[:, :], plc[:, m.slot2, g:g + 1], None,
                                                   ALU.is_equal)
                        last.then_inc(L.sel, 1)
                        dve.wait_ge(L.an, NBLK * m.n + q + 1)
                        xs = xn[:, m.slot4, q * BG:(q + 1) * BG, :]
                        v.tensor_tensor(xs, xs, own[:, m.slot2, q * BG:(q + 1) * BG, :], ALU.add).then_inc(L.second, 1)
                    if q > 0:
                        f = q - 1
                        dve.wait_ge(L.second, NBLK * m.n + f + 1)
                        dve.wait_ge(L.y, NBLK * m.n + f + 1)
                        xs = xn[:, m.slot4, f * BG:(f + 1) * BG, :].rearrange("p a b -> p (a b)")
                        v.tensor_tensor(xs, xs, y_p[:, f % 2, :], ALU.add).then_inc(L.yfree, 1)

            dve.wait_ge(k_free, NK + 1)
            v.memset(alpha[:, 1, 0:1], 0.0).then_inc(L1.yfree, 2)
            v.memset(alpha[:, 1, 1:2], 0.0).then_inc(L2.yfree, 2)
            run(v.Fori, first1, second1)
            dve.wait_ge(L1.second, K_SECOND * NSB)
            run(v.Fori, first2, second2)

        @block.scalar
        def _(act):
            a = nc.scalar.activation

            def rstds(L, t):
                dve_done = t.n + 1
                act.wait_ge(L.var, dve_done)
                a(lnv[:, :], var[:, :], ACT.Ln).then_inc(L.act, 1)
                act.wait_ge(L.act, t.n + 1)
                a(rstd0[:, :], lnv[:, :], ACT.Exp, scale=-0.5).then_inc(L.rstd0, 1)
                act.wait_ge(L.rstd, t.n + 1)

            def first1(t, m):
                L = L1
                rstds(L, t)
                for q in range(NBLK + 1):
                    if q < NBLK:
                        wait(act, L.te, NBLK * t.n + q - 1)
                        for j in range(BG):
                            g = q * BG + j
                            last = a(ae[:, q % 2, j, :], xe[:, t.slot2, g, :], ACT.Identity, bias=nbias[:, g:g + 1],
                                     scale=rstd[:, g:g + 1])
                        last.then_inc(L.ae, 1)
                        act.wait_ge(L.tn, NBLK * t.n + q + 1)
                        wait(act, L.y, NBLK * (t.n - 1))
                        a(hnT[:, t.slot2, q * BG * P:(q + 1) * BG * P], tn_p[:, :], ACT.Relu).then_inc(L.hn, 1)
                    if q == NBLK:
                        messages_out(t, 0)
                    if q > 0:
                        e = q - 1
                        act.wait_ge(L.te, NBLK * t.n + e + 1)
                        wait(act, L.c, NBLK * t.n + e - 1)
                        a(heT[:, e % 2, :], te_p[:, e % 2, :], ACT.Relu).then_inc(L.he, 1)
                    if q == 2 and m is not None:
                        exps1(m)
                for q in range(NBLK):
                    if q < NBLK - 1:
                        messages_out(t, q + 1)
                    if m is not None:
                        slopes1(m, q)

            def messages_out(t, q):
                act.wait_ge(L1.c, NBLK * t.n + q + 1)
                a(cs[:, t.slot2, q * BG:(q + 1) * BG, :].rearrange("p (a b) c -> p a (b c)", a=2),
                  c_p[:, :, 0:2 * (D + 1)], ACT.Copy).then_inc(L1.cs, 1)

            def exps1(m):
                act.wait_ge(L1.d, m.n + 1)
                a(rows[0:GS, 3, :], rows[0:GS, 2, :], ACT.Exp).then_inc(L1.w, 1)

            def slopes1(m, q):
                act.wait_ge(L1.y, NBLK * m.n + q + 1)
                wait(act, L1.yfree, NBLK * m.n + q + 1)
                a(qc[:, q % 2, :], y_p[:, q % 2, :], ACT.Copy, scale=SLOPE).then_inc(L1.qc, 1)

            def second1(m):
                exps1(m)
                for q in range(NBLK):
                    slopes1(m, q)

            def first2(t, m):
                L = L2
                rstds(L, t)
                wait(act, L.y, NBLK * (t.n - 1))
                wait(act, L.second, NBLK * (t.n - 1))
                for q in range(NBLK):
                    for j in range(BG):
                        g = q * BG + j
                        last = a(h2[:, t.slot2, g, :], xe[:, t.slot2, g, :], ACT.Relu, bias=nbias[:, g:g + 1],
                                 scale=rstd[:, g:g + 1])
                    last.then_inc(L.ae, 1)
                for q in range(NBLK):
                    for j in range(BG):
                        g = q * BG + j
                        last = a(own[:, t.slot2, g, :], xn[:, t.slot4, g, :], ACT.Relu, bias=nbias[:, GS + g:GS + g + 1],
                                 scale=rstd[:, GS + g:GS + g + 1])
                    last.then_inc(L.an, 1)

            nc.scalar.preload_act_table_set("natural_log_exp_and_others")
            run(nc.scalar.Fori, first1, second1)
            run(nc.scalar.Fori, first2, lambda m: None)

        @block.tensor
        def _(pe):
            mm, tr = nc.tensor.matmul, nc.tensor.transpose

            def messages(t, q):
                L = L1
                pe.wait_ge(L.he, NBLK * t.n + q + 1)
                pe.wait_ge(L.oh, t.n + 1)
                wait(pe, L.cs, NBLK * t.n + q)
                for j in range(BG):
                    s = slice((q * BG + j) * P, (q * BG + j + 1) * P)
                    to = c_p[:, j // 2, (j % 2) * (D + 1):(j % 2 + 1) * (D + 1)]
                    mm(to, heT[:, q % 2, j * P:(j + 1) * P], w1a[:, :], start=True, stop=False)
                    for part in range(3):
                        mm(to, ota[:, t.slot2, s], rel3[:, 0, part, :], start=False, stop=False)
                    for part in range(3):
                        last = mm(to, otb[0:RB, t.slot2, s], rel3[0:RB, 1, part, :], start=False, stop=part == 2)
                last.then_inc(L.c, 1)

            def aggregate1(m, q):
                L = L1
                pe.wait_ge(L.sel, NBLK * m.n + q + 1)
                pe.wait_ge(L.yfree, NBLK * m.n + q + 1)
                for j in range(BG):
                    g = q * BG + j
                    to = y_p[:, q % 2, j * D:(j + 1) * D]
                    mm(to, hnT[:, m.slot2, g * P:(g + 1) * P], w1s[:, 1, :], start=True, stop=False)
                    mm(to, sel[:, q % 2, j, :], cs[:, m.slot2, g, 0:D], start=False, stop=True)
                wait(pe, L.hasr, NBLK * m.n + q)
                for j in range(BG):
                    last = mm(has_p[:, q, j:j + 1], sel[:, q % 2, j, :], ones[:, :], start=True, stop=True)
                last.then_inc(L.y, 1)

            def scores_to_rows(m):
                pe.wait_ge(L1.b, m.n + 1)
                tr(bT_p, sc[:, 2, :], ident[:, :]).then_inc(L1.bT, 1)

            def weights_to_columns(m):
                pe.wait_ge(L1.al, m.n + 1)
                mm(alT_p, rows[:, 7, :], ident[:, 0:GS], start=True, stop=True).then_inc(L1.alT, 1)

            def node_scores(t, has_read):
                L = L1
                wait(pe, L.hasr, has_read)
                pe.wait_ge(L.hn, NBLK * (t.n + 1))
                wait(pe, L.sn3, t.n)
                for g in range(GS):
                    last = mm(sn_p[:, g:g + 1], hnT[:, t.slot2, g * P:(g + 1) * P], ub[:, :], start=True, stop=True)
                last.then_inc(L.sn, 1)

            def destination_scores(t):
                L = L1
                pe.wait_ge(L.sn3, t.n + 1)
                wait(pe, L.b, t.n)
                for g in range(GS):
                    last = mm(sd_p[:, 3 * g:3 * g + 3], selT[:, t.slot2, g * P:(g + 1) * P], sn3[:, g, :], start=True, stop=True)
                last.then_inc(L.sd, 1)

            def first1(t, m):
                L = L1
                for q in range(NBLK):
                    pe.wait_ge(L.an, NBLK * t.n + q + 1)
                    wait(pe, L.hn, NBLK * t.n + q)
                    for j in range(BG):
                        last = tr(tn_p[:, j * P:(j + 1) * P], an[:, q % 2, j, :], ident[:, :])
                    last.then_inc(L.tn, 1)
                    pe.wait_ge(L.ae, NBLK * t.n + q + 1)
                    wait(pe, L.he, NBLK * t.n + q - 1)
                    for j in range(BG):
                        last = tr(te_p[:, q % 2, j * P:(j + 1) * P], ae[:, q % 2, j, :], ident[:, :])
                    last.then_inc(L.te, 1)
                    if q == 2:
                        messages(t, 0)
                        if m is not None:
                            scores_to_rows(m)
                    if q == 3:
                        messages(t, 1)
                if m is not None:
                    weights_to_columns(m)
                    messages(t, 2)
                    aggregate1(m, 0)
                    messages(t, 3)
                    aggregate1(m, 1)
                    node_scores(t, NBLK * m.n + 2)
                    aggregate1(m, 2)
                    aggregate1(m, 3)
                else:
                    messages(t, 2)
                    messages(t, 3)
                    node_scores(t, 0)
                destination_scores(t)

            def second1(m):
                scores_to_rows(m)
                weights_to_columns(m)
                for q in range(NBLK):
                    aggregate1(m, q)

            def first2(t, m):
                if m is not None:
                    second2(m)

            def second2(m):
                L = L2
                pe.wait_ge(L.ae, NBLK * (m.n + 1))
                for q in range(NBLK):
                    pe.wait_ge(L.sel, NBLK * m.n + q + 1)
                    pe.wait_ge(L.yfree, NBLK * m.n + q + 1)
                    for j in range(BG):
                        last = mm(y_p[:, q % 2, j * D:(j + 1) * D], sel[:, q % 2, j, :], h2[:, m.slot2, q * BG + j, :],
                                  start=True, stop=True)
                    last.then_inc(L.y, 1)

            run(nc.tensor.Fori, first1, second1)
            run(nc.tensor.Fori, first2, second2)


def kernel(x, src, dst, edge_type_200, L0_gnn_relation_embedding, L0_gnn_W1, L0_gnn_b1, L0_gnn_w2):
    import numpy as np
    import concourse.bacc as bacc
    from concourse.bass_utils import run_bass_kernel_spmd

    nc = bacc.Bacc("TRN2", target_bir_lowering=False, num_devices=1)
    n_edges, n_nodes = src.shape[0], x.shape[0]
    width = -(-(n_edges + P) // (4 * P)) * 4 * P

    def padded(a, end):
        return np.concatenate([a, np.full(width - n_edges, end, a.dtype)]).reshape(1, width)

    arrays = {"x": np.ascontiguousarray(x), "src": padded(src, 0), "dst": padded(dst, 2 * n_nodes),
              "typ": padded(edge_type_200, 0), "rel": np.ascontiguousarray(L0_gnn_relation_embedding),
              "w1": np.ascontiguousarray(L0_gnn_W1), "b1": np.ascontiguousarray(L0_gnn_b1), "w2": np.ascontiguousarray(L0_gnn_w2)}
    args = [nc.dram_tensor(f"in_{k}", a.shape, mybir.dt.from_np(a.dtype), kind="ExternalInput").ap() for k, a in arrays.items()]
    out = nc.dram_tensor("out", x.shape, mybir.dt.float32, kind="ExternalOutput").ap()
    gnn_two_layers(nc, *args, out)
    r = run_bass_kernel_spmd(nc, [{f"in_{k}": a for k, a in arrays.items()}], core_ids=[0])
    return r.results[0]["out"]
```

```python
import concourse.bass as bass
from concourse import mybir
from contextlib import ExitStack

P = 128
D = 128
GS = 16
BG = 4
NBLK = GS // BG
EPS = 1e-5
SLOPE = 0.01
FAR = float(2.0 ** 100)
SKIP = float(2 ** 20)
OFF = 200.0


def wait(engine, semaphore, value):
    if isinstance(value, int) and value <= 0:
        return
    engine.wait_ge(semaphore, value)


class At:

    def __init__(self, i, k):
        self.n = 4 * i + k
        self.slot4, self.round4 = k % 4, i + k // 4
        self.slot2, self.round2 = k % 2, 2 * i + k // 2


class Semaphores:

    def __init__(self, sem, n):
        def several(name, count):
            return [sem(f"{name}{s}_{n}") for s in range(count)]

        self.x_in = several("x_in", 4)
        self.rest_in = sem(f"rest_in_{n}")
        self.idx_in = several("idx_in", 4)
        self.rows_in = several("rows_in", 4)
        self.gathered = several("gathered", 4)
        self.stored = several("stored", 4)
        self.turns = sem(f"turns_{n}")
        self.row_turns = sem(f"row_turns_{n}")
        self.var = sem(f"var_{n}")
        self.ln = sem(f"ln_{n}")
        self.rstd0 = sem(f"rstd0_{n}")
        self.rstd = sem(f"rstd_{n}")
        self.ae = sem(f"ae_{n}")
        self.an = sem(f"an_{n}")
        self.sel = sem(f"sel_{n}")
        self.y = sem(f"y_{n}")
        self.yfree = sem(f"yfree_{n}")
        self.x1 = sem(f"x1_{n}")
        self.first = sem(f"first_{n}")
        self.second = sem(f"second_{n}")
        if n == 2:
            return
        self.tables_in = several("tables_in", 2)
        self.tn = sem("tn")
        self.te = sem("te")
        self.hn = sem("hn")
        self.he = sem("he")
        self.oh = sem("oh")
        self.c = sem("c")
        self.cs = sem("cs")
        self.split = sem("split")
        self.sn3 = sem("sn3")
        self.sd = sem("sd")
        self.b = sem("b")
        self.bT = sem("bT")
        self.d = sem("d")
        self.w = sem("w")
        self.al = sem("al")
        self.alT = sem("alT")
        self.qc = sem("qc")
        self.has_turns = sem("has_turns")
        self.has = sem("has")


class Steps:

    def __init__(self, engine, semaphore, done):
        self.engine, self.semaphore, self.done = engine, semaphore, done
        self.n = 0

    def mark(self, instruction):
        self.n += 1
        instruction.then_inc(self.semaphore, 1)

    def settle(self):
        self.engine.wait_ge(self.semaphore, self.done + self.n)

    def then(self, instruction):
        self.mark(instruction)
        self.settle()


def gnn_two_layers(nc, x, src_e, dst_e, typ_e, rel, w1, b1, w2, out):
    f32, bf16, i32, u32 = mybir.dt.float32, mybir.dt.bfloat16, mybir.dt.int32, mybir.dt.uint32
    ALU, ACT, AX = mybir.AluOpType, mybir.ActivationFunctionType, mybir.AxisListType.X

    N = x.shape[0]
    EC = dst_e.shape[1] // P
    R = rel.shape[0]
    RB = R - P
    NSB = -(-N // (GS * P))
    NG = NSB * GS
    NK = -(-NG // P)
    LOOPS = (NSB - 1) // 4
    assert NSB == 4 * LOOPS + 1 and EC % 4 == 0
    TAIL = N - (NSB - 1) * GS * P
    TG, TR = TAIL // P, TAIL % P
    assert TG > 1

    starts_d = nc.dram_tensor("starts_d", (1024, 1), i32, kind="Internal").ap()
    scan_d = nc.dram_tensor("scan_d", (NK * P, 4 * P), f32, kind="Internal").ap()
    place_d = nc.dram_tensor("place_d", (NK * P, P), bf16, kind="Internal").ap()
    types_d = nc.dram_tensor("types_d", (NK * P, P), bf16, kind="Internal").ap()
    x1_d = nc.dram_tensor("x1_d", (N, D), f32, kind="Internal").ap()

    ctx = ExitStack()
    with ctx:
        def sb(name, shape, dt):
            return ctx.enter_context(nc.sbuf_tensor(name, shape, dt))

        def pb(name, shape, dt):
            return ctx.enter_context(nc.psum_tensor(name, shape, dt))

        def sem(name):
            return ctx.enter_context(nc.semaphore(name))

        ident = sb("ident", [P, P], f32)
        row = sb("row", [P, P], f32)
        col = sb("col", [P, 2], f32)
        gbase = sb("gbase", [P, NK], f32)
        fold = sb("fold", [P, 32], f32)
        below = sb("below", [32, 32], f32)
        blocks4 = sb("blocks4", [P, 4], f32)
        row32 = sb("row32", [P, 32], f32)
        ones = sb("ones", [P, 1], f32)
        w1s = sb("w1s", [P, 3, D], f32)
        w2b = sb("w2b", [P, D], f32)
        b1b = sb("b1b", [P, D], f32)
        rels = sb("rels", [P, 2, D], f32)
        relT = sb("relT", [P, 2 * P], f32)
        w1a = sb("w1a", [P, D + 1], f32)
        ub = sb("ub", [P, 1], f32)
        relw = sb("relw", [P, 2, D + 1], f32)
        rel3 = sb("rel3", [P, 2, 3, D + 1], bf16)
        junk = sb("junk", [P, D + 1], f32)

        idx_t = sb("idx_t", [P, NK * P], u32)
        plc_t = sb("plc_t", [P, NK * P], f32)
        has_t = sb("has_t", [P, NG], f32)

        xn = sb("xn", [P, 4, GS, D], f32)
        xe = sb("xe", [P, 4, GS, D], f32)
        an = sb("an", [P, 2, BG, D], f32)
        ae = sb("ae", [P, 2, BG, D], f32)
        heT = sb("heT", [P, 2, BG * P], f32)
        hnT = sb("hnT", [P, 2, GS * P], f32)
        cs = sb("cs", [P, 2, GS, D + 2], f32)
        sel = sb("sel", [P, 2, BG, P], f32)
        plr = sb("plr", [P, 2, GS * P], bf16)
        tyr = sb("tyr", [P, 2, GS * P], bf16)
        ota = sb("ota", [P, 2, GS * P], bf16)
        otb = sb("otb", [P, 2, GS * P], bf16)
        selT = sb("selT", [P, 2, GS * P], bf16)
        scn = sb("scn", [GS, 4, 4, P], f32)
        plc = sb("plc", [P, 4, GS], f32)
        idx = sb("idx", [P, 4, GS], u32)
        qc = sb("qc", [P, 2, BG * D], f32)
        lr = sb("lr", [P, 2, BG * D], f32)
        st = sb("st", [P, 2 * GS, 6], f32)
        tiny = sb("tiny", [P, 12, 2 * GS], f32)
        rstd0 = sb("rstd0", [P, 2 * GS], f32)
        lnv = sb("lnv", [P, 2 * GS], f32)
        var = sb("var", [P, 2 * GS], f32)
        rstd = sb("rstd", [P, 2, 2 * GS], f32)
        nbias = sb("nbias", [P, 2, 2 * GS], f32)
        sn3 = sb("sn3", [P, GS, 3], bf16)
        snr = sb("snr", [P, 2, GS], f32)
        sc = sb("sc", [P, 3, GS], f32)
        rows = sb("rows", [P, 8, P], f32)
        alpha = sb("alpha", [P, 2, GS], f32)
        half = sb("half", [P, GS, 64], bf16)[:, :, :]
        quarter = sb("quarter", [P, GS, 32], bf16)[:, :, :]
        some = sb("some", [P, 2, GS, 16], bf16)

        tn_p = pb("tn_p", [P, BG * P], f32)
        te_p = pb("te_p", [P, 2, BG * P], f32)
        c_p = pb("c_p", [P, 2, 512], f32)
        y_p = pb("y_p", [P, 2, BG * D], f32)
        s_p = pb("s_p", [P, 512], f32)
        sd_p = s_p[:, 0:3 * GS]
        bT_p, alT_p = s_p[0:GS, 64:64 + P], s_p[:, 192:192 + GS]

        k_in = sem("k_in")
        k_const = sem("k_const")
        k_pool = sem("k_pool")
        k_dve = sem("k_dve")
        k_pe = sem("k_pe")
        k_start = sem("k_start")
        k_startl = sem("k_startl")
        k_gat = [sem(f"k_gat{i}") for i in range(2)]
        k_free = sem("k_free")
        k_idx = sem("k_idx")
        k_tr = sem("k_tr")
        k_out = [sem(f"k_out{i}") for i in range(2)]
        k_rows = sem("k_rows")

        with ExitStack() as ctx1:
            dsti = xn[:, 0, 0:4, :].rearrange("p a b -> p (a b)")[:, 0:EC].bitcast(i32)
            hi_i = xn[:, 0, 4:8, :].rearrange("p a b -> p (a b)")[:, 0:EC].bitcast(i32)
            lo_i = xn[:, 0, 8:12, :].rearrange("p a b -> p (a b)")[:, 0:EC].bitcast(i32)
            hi_f = xn[:, 1, 0:4, :].rearrange("p a b -> p (a b)")[:, 0:EC]
            lo_f = xn[:, 1, 4:8, :].rearrange("p a b -> p (a b)")[:, 0:EC]
            CH = EC // 4
            oh_h = hnT[:, :, :].rearrange("p a b -> p (a b)").bitcast(bf16)[:, 0:CH * 32].rearrange("p (c h) -> p c h", h=32)
            oh_l = cs[:, 0, :, :].rearrange("p a b -> p (a b)").bitcast(bf16)[:, 0:CH * 32].rearrange("p (c h) -> p c h", h=32)
            hist_p = tn_p[:, 0:P]
            cnt_p = tn_p[0:32, 128:160]
            pre_p = tn_p[0:32, 160:161]
            histm = sel[:, 0, 0, :]
            histr = sel[:, 0, 1, 0:32]
            cnt = sel[0:32, 0, 2, 0:32]
            cum = sel[0:32, 0, 2, 32:64]
            pre = sel[0:32, 0, 2, 64:65]
            zero32 = sel[0:32, 0, 2, 96:128]
            sta = sel[0:32, 0, 3, 0:32]
            stai = sel[0:32, 0, 3, 32:64].bitcast(i32)
            first = lr[:, 0, 0:NK].bitcast(i32)
            gd = [xe[:, i, 0, :].bitcast(i32) for i in range(2)]
            gs_ = [xe[:, i, 1, :].bitcast(i32) for i in range(2)]
            gt = [xe[:, i, 2, :].bitcast(i32) for i in range(2)]
            plf = [xe[:, i, 3, :] for i in range(2)]
            idf = [xe[:, i, 4, :] for i in range(2)]
            srf = [xe[:, i, 5, :] for i in range(2)]
            mf = [xe[:, i, 6:10, :] for i in range(2)]
            plb = [xe[:, i, 10, 0:64].bitcast(bf16) for i in range(2)]
            tyb = [xe[:, i, 11, 0:64].bitcast(bf16) for i in range(2)]

            block = ctx1.enter_context(nc.Block())
            NIN = 6

            @block.sync
            def _(sp):
                sp.dma_start(dsti, dst_e.rearrange("o (p c) -> (o p) c", p=P)).then_inc(k_in, 16)
                sp.dma_start(w1s[:, :, :], w1.rearrange("(a p) d -> p a d", p=P)).then_inc(k_in, 16)
                sp.dma_start(rels[:, 0, :], rel[0:P, :]).then_inc(k_in, 16)
                sp.dma_start(rels[0:RB, 1, :], rel[P:R, :]).then_inc(k_in, 16)
                sp.dma_start(w2b[:, :], w2.partition_broadcast(P)).then_inc(k_in, 16)
                sp.dma_start(b1b[:, :], b1.partition_broadcast(P)).then_inc(k_in, 16)
                sp.wait_ge(k_start, 1)
                sp.dma_start(starts_d.rearrange("(h l) o -> h (l o)", l=32), stai).then_inc(k_startl, 16)
                sp.wait_ge(k_startl, 16)
                sp.dma_start(first, starts_d[0:NK * P, :].rearrange("(k p) o -> p (k o)", p=P),
                             allow_slow_non_contiguous=True).then_inc(k_startl, 16)
                for k in range(NK):
                    sp.wait_ge(k_rows, k + 1)
                    for table, made in ((scan_d, mf[k % 2].rearrange("p a b -> p (a b)")), (place_d, plb[k % 2]), (types_d, tyb[k % 2])):
                        sp.dma_start(table[k * P:(k + 1) * P, :], made).then_inc(k_out[k % 2], 16)
                for i in range(2):
                    sp.wait_ge(k_out[i], 48 * ((NK + 1 - i) // 2))

            @block.gpsimd
            def _(pool):
                g = nc.gpsimd
                steps = Steps(pool, k_pool, 0)
                g.iota(row[:, :], pattern=[[1, P]], base=0, channel_multiplier=0, allow_small_or_imprecise_dtypes=True)
                g.iota(row32[:, :], pattern=[[1, 32]], base=0, channel_multiplier=0, allow_small_or_imprecise_dtypes=True)
                g.iota(col[:, :], pattern=[[P, 2]], base=0, channel_multiplier=1, allow_small_or_imprecise_dtypes=True)
                g.iota(gbase[:, :], pattern=[[P * P, NK]], base=0, channel_multiplier=P, allow_small_or_imprecise_dtypes=True)
                g.memset(ident[:, :], 0.0)
                g.memset(ones[:, :], 1.0)
                g.memset(fold[:, :], 0.0)
                g.memset(below[:, :], 1.0)
                steps.then(g.memset(blocks4[:, :], 1.0))
                g.affine_select(out=ident[:, :], in_=ident[:, :], compare_op=ALU.not_equal, fill=1.0, base=0,
                                pattern=[[-1, P]], channel_multiplier=1)
                g.affine_select(out=below[:, :], in_=below[:, :], compare_op=ALU.is_gt, fill=0.0, base=0,
                                pattern=[[1, 32]], channel_multiplier=-1)
                steps.then(g.affine_select(out=blocks4[:, :], in_=blocks4[:, :], compare_op=ALU.is_ge, fill=0.0, base=0,
                                           pattern=[[-32, 4]], channel_multiplier=1))
                steps.then(g.affine_select(out=blocks4[:, :], in_=blocks4[:, :], compare_op=ALU.is_ge, fill=0.0, base=31,
                                           pattern=[[32, 4]], channel_multiplier=-1))
                for a in range(4):
                    steps.then(g.affine_select(out=fold[:, :], in_=fold[:, :], compare_op=ALU.not_equal, fill=1.0,
                                               base=-32 * a, pattern=[[-1, 32]], channel_multiplier=1))
                g.memset(zero32, 0.0).then_inc(k_const, 1)
                pool.wait_ge(k_startl, 32)
                for k in range(NK):
                    wait(pool, k_free, k - 1)
                    for to, e in ((gs_, src_e), (gd, dst_e), (gt, typ_e)):
                        g.indirect_dma_start(out=to[k % 2], out_offset=None, in_=e,
                                             in_offset=bass.IndirectOffsetOnAxis(ap=first[:, k:k + 1].bitcast(u32), axis=1)
                                             ).then_inc(k_gat[k % 2], 16)

            @block.tensor
            def _(pe):
                pe.wait_ge(k_const, 1)
                pe.wait_ge(k_in, 16 * NIN)
                nc.tensor.transpose(te_p[:, 0, 0:P], rels[:, 0, :], ident[:, :])
                nc.tensor.transpose(te_p[:, 0, P:P + RB], rels[0:RB, 1, :], ident[0:RB, 0:RB]).then_inc(k_pe, 1)
                for c in range(4):
                    pe.wait_ge(k_idx, c + 1)
                    for j in range(CH // 4 + (CH % 4 > 0)):
                        w = min(4, CH - 4 * j)
                        last = nc.tensor.matmul(hist_p[0:32 * w, 0:32 * w],
                                                oh_h[:, 4 * j:4 * j + w, :].rearrange("p c h -> p (c h)"),
                                                oh_l[:, 4 * j:4 * j + w, :].rearrange("p c h -> p (c h)"),
                                                start=(c == 0 and j == 0), stop=(c == 3 and 4 * j + w == CH),
                                                skip_group_check=True)
                    last.then_inc(k_tr, 1)
                pe.wait_ge(k_idx, 5)
                nc.tensor.matmul(cnt_p, fold[:, :], histr, start=True, stop=True).then_inc(k_tr, 1)
                pe.wait_ge(k_idx, 6)
                nc.tensor.matmul(pre_p, below[:, :], cum[:, 31:32], start=True, stop=True).then_inc(k_tr, 1)
                pe.wait_ge(k_idx, 7)
                nc.tensor.matmul(te_p[:, 1, 0:P], relT[:, 0:P], w1s[:, 2, :], start=True, stop=True)
                nc.tensor.matmul(te_p[0:RB, 1, P:2 * P], relT[:, P:P + RB], w1s[:, 2, :], start=True, stop=True).then_inc(k_tr, 1)
                for k in range(NK):
                    pe.wait_ge(k_rows, k + 1)
                    wait(pe, k_free, k - 1)
                    nc.tensor.transpose(c_p[:, k % 2, 0:P], idf[k % 2], ident[:, :])
                    nc.tensor.transpose(c_p[:, k % 2, P:2 * P], plf[k % 2], ident[:, :]).then_inc(k_pe, 1)

            @block.vector
            def _(dve):
                v = nc.vector
                steps = Steps(dve, k_dve, 0)
                dve.wait_ge(k_in, 16 * NIN)
                dve.wait_ge(k_const, 1)
                v.tensor_scalar(hi_i, dsti, 12, None, ALU.logical_shift_right)
                steps.then(v.tensor_scalar(lo_i, dsti, 20, 27, ALU.logical_shift_left, ALU.logical_shift_right))
                v.tensor_copy(hi_f, hi_i)
                steps.then(v.tensor_copy(lo_f, lo_i))
                for c in range(4):
                    wait(dve, k_tr, c)
                    r32 = row32[:, :].unsqueeze(1).to_broadcast([P, CH, 32])
                    v.tensor_tensor(oh_h, hi_f[:, c * CH:(c + 1) * CH].unsqueeze(2).to_broadcast([P, CH, 32]), r32, ALU.is_equal)
                    v.tensor_tensor(oh_l, lo_f[:, c * CH:(c + 1) * CH].unsqueeze(2).to_broadcast([P, CH, 32]), r32,
                                    ALU.is_equal).then_inc(k_idx, 1)
                dve.wait_ge(k_tr, 4)
                steps.then(v.tensor_tensor(histm.rearrange("p (a l) -> p a l", a=4), hist_p.rearrange("p (a l) -> p a l", a=4),
                                           blocks4[:, :].unsqueeze(2).to_broadcast([P, 4, 32]), ALU.mult))
                v.tensor_reduce(histr, histm.rearrange("p (a l) -> p l a", a=4), AX, ALU.add).then_inc(k_idx, 1)
                dve.wait_ge(k_tr, 5)
                steps.then(v.tensor_copy(cnt, cnt_p))
                v.tensor_tensor_scan(cum, zero32, cnt, 0.0, ALU.add, ALU.add).then_inc(k_idx, 1)
                dve.wait_ge(k_idx, 6)
                dve.wait_ge(k_tr, 6)
                steps.then(v.tensor_copy(pre, pre_p))
                steps.then(v.scalar_tensor_tensor(sta, cum, pre, cnt, ALU.add, ALU.subtract))
                v.tensor_copy(stai, sta).then_inc(k_start, 1)
                dve.wait_ge(k_pe, 1)
                v.tensor_copy(relT[:, 0:P + RB], te_p[:, 0, 0:P + RB]).then_inc(k_idx, 1)
                v.tensor_copy(w1a[:, 0:D], w1s[:, 0, :])

                def dot_w2(into, a, n):
                    steps.then(v.tensor_tensor_reduce(out=junk[0:n, 0:D], in0=a, in1=w2b[0:n, :], scale=1.0, scalar=0.0,
                                                      op0=ALU.mult, op1=ALU.add, accum_out=into))

                dot_w2(w1a[:, D:D + 1], w1s[:, 0, :], P)
                dot_w2(ub[:, :], w1s[:, 1, :], P)
                dve.wait_ge(k_tr, 7)
                for c, n in ((0, P), (1, RB)):
                    steps.then(v.tensor_tensor(relw[0:n, c, 0:D], te_p[0:n, 1, c * P:c * P + D], b1b[0:n, :], ALU.add))
                    dot_w2(relw[0:n, c, D:D + 1], relw[0:n, c, 0:D], n)
                    steps.then(v.tensor_copy(rel3[0:n, c, 0, :], relw[0:n, c, :]))
                    steps.then(v.tensor_tensor(junk[0:n, :], relw[0:n, c, :], rel3[0:n, c, 0, :], ALU.subtract))
                    steps.then(v.tensor_copy(rel3[0:n, c, 1, :], junk[0:n, :]))
                    steps.then(v.tensor_tensor(rel3[0:n, c, 2, :], junk[0:n, :], rel3[0:n, c, 1, :], ALU.subtract))
                for k in range(NK):
                    i = k % 2
                    dve.wait_ge(k_gat[i], 48 * (k // 2 + 1))
                    wait(dve, k_out[i], 48 * (k // 2))
                    p, m = plf[i], mf[i]
                    v.tensor_copy(srf[i], gs_[i])
                    v.tensor_copy(tyb[i], gt[i])
                    steps.then(v.tensor_copy(p, gd[i]))
                    steps.then(v.tensor_scalar(p, p, gbase[:, k:k + 1], OFF, ALU.subtract, ALU.min))
                    v.tensor_copy(plb[i], p)
                    v.tensor_scalar(idf[i], p, float(P - 1), SKIP, ALU.is_gt, ALU.mult)
                    v.memset(m[:, 2, 0:1], 0.0)
                    v.memset(m[:, 3, P - 1:P], 0.0)
                    v.tensor_tensor(m[:, 2, 1:P], p[:, 1:P], p[:, 0:P - 1], ALU.is_equal)
                    steps.then(v.tensor_tensor(m[:, 3, 0:P - 1], p[:, 0:P - 1], p[:, 1:P], ALU.is_equal))
                    v.tensor_scalar(m[:, 0:2, :], m[:, 2:4, :], 1.0, FAR, ALU.subtract, ALU.mult)
                    v.tensor_tensor(idf[i], idf[i], srf[i], ALU.add).then_inc(k_rows, 1)
                    dve.wait_ge(k_pe, k + 2)
                    v.tensor_copy(idx_t[:, k * P:(k + 1) * P], c_p[:, i, 0:P])
                    v.tensor_copy(plc_t[:, k * P:(k + 1) * P], c_p[:, i, P:2 * P]).then_inc(k_free, 1)
                dve.wait_ge(k_free, NK)
                for i in range(2):
                    dve.wait_ge(k_out[i], 48 * ((NK + 1 - i) // 2))
                v.memset(xe[:, :, :, :], 0.0)
                v.memset(rows[:, :, :], 0.0)
                for i in range(4):
                    last = v.memset(xn[:, i, :, :], 0.0)
                last.then_inc(k_free, 1)

        L1, L2 = Semaphores(sem, 1), Semaphores(sem, 2)

        block = ctx.enter_context(nc.Block())

        def nodes_of(a, t, tail):
            if not tail:
                half = GS // 2
                return [(a[bass.ds(t.n * GS * P + h * half * P, half * P), :].rearrange("(g p) d -> p g d", p=P),
                         h * half, (h + 1) * half, P) for h in range(2)]
            at = (NSB - 1) * GS * P
            parts = []
            if TG:
                half = TG // 2
                for g0, g1 in ((0, half), (half, TG)):
                    parts.append((a[at + g0 * P:at + g1 * P, :].rearrange("(g p) d -> p g d", p=P), g0, g1, P))
            if TR:
                parts.append((a[at + TG * P:N, :].rearrange("(g p) d -> p g d", p=TR), TG, TG + 1, TR))
            return parts

        NTAIL = 2 + (TR > 0)

        @block.sync
        def _(sp):
            def done(L, n):
                if L is L1:
                    wait(sp, L1.x1, n)
                elif not (isinstance(n, int) and n <= 0):
                    sp.wait_ge(L2.yfree, 2 + NBLK * n)

            def load_x(L, a, t, tail=False):
                wait(sp, L.stored[t.slot4], 32 * t.round4)
                first, second, *rest = nodes_of(a, t, tail)
                for r_rows, r0, r1, r_np in rest:
                    sp.dma_start(xn[0:r_np, t.slot4, r0:r1, :], r_rows).then_inc(L.rest_in, 16)
                    sp.wait_ge(L.rest_in, 16)
                for rows_, g0, g1, np_ in (first, second):
                    sp.dma_start(xn[0:np_, t.slot4, g0:g1, :], rows_).then_inc(L.x_in[t.slot4], 16)

            def load_idx(L, t):
                wait(sp, L.gathered[t.slot4], 256 * t.round4)
                sp.dma_start(idx[:, t.slot4, :], idx_t[:, bass.ds(t.n * GS, GS)]).then_inc(L.idx_in[t.slot4], 16)

            def load_rows(L, n, t):
                done(L, t.n - 3)
                sp.sem_inc(L.row_turns, 1)
                sp.dma_start(plc[:, t.slot4, :], plc_t[:, bass.ds(t.n * GS, GS)]).then_inc(L.rows_in[t.slot4], 16)
                if n == 1:
                    sp.dma_start(scn[:, t.slot4, :, :].rearrange("g a b -> g (a b)"),
                                 scan_d[bass.ds(t.n * GS, GS), :]).then_inc(L.rows_in[t.slot4], 16)

            def load_tables(t):
                wait(sp, L1.oh, t.n - 1)
                sp.sem_inc(L1.row_turns, 1)
                for to, table in ((plr, place_d), (tyr, types_d)):
                    sp.dma_start(to[:, t.slot2, :],
                                 table[bass.ds(t.n * GS, GS), :].rearrange("g s -> (g s)").partition_broadcast(P)
                                 ).then_inc(L1.tables_in[t.slot2], 16)

            def store(L, a, t, tail=False):
                done(L, t.n + 1)
                for rows_, g0, g1, np_ in nodes_of(a, t, tail):
                    sp.dma_start(rows_, xn[0:np_, t.slot4, g0:g1, :]).then_inc(L.stored[t.slot4], 16)

            def layer(L, n, a, to):
                def load(t, tail=False):
                    load_x(L, a, t, tail)
                    load_idx(L, t)
                    load_rows(L, n, t)
                    if n == 1:
                        load_tables(t)

                def turn(i, k, last=False):
                    if not last or k < 2:
                        load(At(i, k + 3), tail=last and k == 1)
                    store(L, to, At(i, k))

                for k in range(3):
                    load(At(0, k))
                for k in range(4):
                    turn(0, k)
                with nc.sync.Fori(1, LOOPS - 1) as i:
                    for k in range(4):
                        turn(i, k)
                for k in range(4):
                    turn(LOOPS - 1, k, last=True)
                store(L, to, At(LOOPS, 0), tail=True)
                for s in range(4):
                    sp.wait_ge(L.stored[s], 32 * LOOPS + (16 * NTAIL if s == 0 else 0))

            sp.wait_ge(k_free, NK + 1)
            layer(L1, 1, x, x1_d)
            layer(L2, 2, x1_d, out)

        @block.gpsimd
        def _(pool):
            def gather(L, a, t):
                wait(pool, L.idx_in[t.slot4], 16 * (t.round4 + 1))
                wait(pool, L.ae, NBLK * (t.n - 3))
                pool.sem_inc(L.turns, 1)
                for j in range(GS):
                    nc.gpsimd.indirect_dma_start(out=xe[:, t.slot4, j, :], out_offset=None, in_=a,
                                                 in_offset=bass.IndirectOffsetOnAxis(ap=idx[:, t.slot4, j:j + 1], axis=0),
                                                 bounds_check=last_row, oob_is_err=False).then_inc(L.gathered[t.slot4], 16)

            pool.wait_ge(k_free, NK + 1)
            last_row = nc.gpsimd.to_reg(N - 1)

            def nodes_with_edges(t):
                pool.wait_ge(L1.oh, t.n + 1)
                wait(pool, L1.rstd, t.n - 1)
                pool.sem_inc(L1.has_turns, 1)
                marks = selT[:, t.slot2, :].rearrange("p (g s) -> p g s", s=P)
                for level, to in enumerate((half, quarter, some[:, t.slot2, :, :])):
                    n = to.shape[2]
                    nc.gpsimd.tensor_tensor(to, marks[:, :, 0:n], marks[:, :, n:2 * n], ALU.add).then_inc(L1.has, 1)
                    pool.wait_ge(L1.has, 3 * t.n + level + 1)
                    marks = to

            for L, a in ((L1, x), (L2, x1_d)):
                if L is L2:
                    for s in range(4):
                        pool.wait_ge(L1.stored[s], 32 * LOOPS + (16 * NTAIL if s == 0 else 0))
                for k in range(5):
                    if L is L1 and k >= 2:
                        nodes_with_edges(At(0, k - 2))
                    gather(L, a, At(0, k))
                with nc.gpsimd.Fori(1, LOOPS) as i:
                    for k in range(1, 5):
                        if L is L1:
                            nodes_with_edges(At(i, k - 2))
                        gather(L, a, At(i, k))
                if L is L1:
                    nodes_with_edges(At(LOOPS, -1))
                    nodes_with_edges(At(LOOPS, 0))

        h2 = hnT[:, :, :].rearrange("p s (g d) -> p s g d", g=GS)
        own = cs[:, :, :, 0:D]

        def run(engine_fori, turn):
            turn(At(0, 0), None, None)
            for k in range(4):
                turn(At(0, k + 1), At(0, k), At(0, k - 1) if k else None)
            with engine_fori(1, LOOPS) as i:
                for k in range(4):
                    turn(At(i, k + 1), At(i, k), At(i, k - 1))
            turn(None, At(LOOPS, 0), At(LOOPS, -1))
            turn(None, None, At(LOOPS, 0))

        @block.vector
        def _(dve):
            v = nc.vector
            SOFT = 8
            K_FIRST = {1: 9, 2: 7}
            K_SECOND = SOFT + NBLK - 1

            def stats_some(L, t, part):
                if t is None:
                    return
                if part == 0:
                    dve.wait_ge(L.x_in[t.slot4], 32 * (t.round4 + 1))
                if part == 4:
                    dve.wait_ge(L.gathered[t.slot4], 256 * (t.round4 + 1))
                for j in range(part % 4 * BG, part % 4 * BG + BG):
                    if part < 4:
                        v.bn_stats(st[:, GS + j, :], xn[:, t.slot4, j, :])
                    else:
                        last = v.bn_stats(st[:, j, :], xe[:, t.slot4, j, :])
                if part == 7:
                    last.then_inc(L.first, 1)

            def variances(L, n, t):
                if t is None:
                    return
                steps = Steps(dve, L.first, K_FIRST[n] * t.n)
                steps.n = 1
                steps.settle()
                msum, dm, m2, dm2, m2e = (tiny[:, c, :] for c in range(5))
                v.tensor_tensor(msum, st[:, :, 1], st[:, :, 4], ALU.add)
                v.tensor_tensor(dm, st[:, :, 1], st[:, :, 4], ALU.subtract)
                steps.then(v.tensor_tensor(m2, st[:, :, 2], st[:, :, 5], ALU.add))
                v.scalar_tensor_tensor(dm2, dm, 0.25, dm, ALU.mult, ALU.mult)
                steps.then(v.tensor_scalar(m2e, m2, 1.0 / D, EPS, ALU.mult, ALU.add))
                v.tensor_tensor(var[:, :], dm2, m2e, ALU.add).then_inc(L.var, 1)

            def factors(L, n, t):
                if t is None:
                    return
                steps = Steps(dve, L.first, K_FIRST[n] * t.n)
                steps.n = 3
                has = has_t[:, bass.ds(t.n * GS, GS)]
                if n == 1:
                    dve.wait_ge(L.has, 3 * (t.n + 1))
                    steps.then(v.tensor_reduce(has, some[:, t.slot2, :, :], AX, ALU.add))
                    steps.then(v.tensor_scalar(has, has, 0.5, None, ALU.is_gt))
                dve.wait_ge(L.rstd0, t.n + 1)
                msum, t0, t1 = tiny[:, 0, :], tiny[:, 5, :], tiny[:, 6, :]
                r = rstd[:, t.slot2, :]
                steps.then(v.tensor_tensor(t0, var[:, :], rstd0[:, :], ALU.mult))
                steps.then(v.scalar_tensor_tensor(t1, t0, -0.5, rstd0[:, :], ALU.mult, ALU.mult))
                wait(dve, L.ae, NBLK * (t.n - 1))
                wait(dve, L.an, NBLK * (t.n - 1))
                if n == 2:
                    v.tensor_scalar(tiny[:, 7, 0:GS], has, -1.0, 1.0, ALU.mult, ALU.add)
                    has = tiny[:, 7, 0:GS]
                steps.then(v.scalar_tensor_tensor(r, t1, 1.5, rstd0[:, :], ALU.add, ALU.mult))
                steps.then(v.tensor_tensor(r[:, GS:2 * GS], r[:, GS:2 * GS], has, ALU.mult))
                v.scalar_tensor_tensor(nbias[:, t.slot2, :], msum, -0.5, r, ALU.mult, ALU.mult).then_inc(L.rstd, 1)
                assert steps.n == K_FIRST[n], steps.n

            def one_hots(t):
                if t is None:
                    return
                L = L1
                dve.wait_ge(L.tables_in[t.slot2], 32 * (t.round2 + 1))
                wait(dve, L.sd, t.n - 1)
                wait(dve, L.c, NBLK * (t.n - 1))
                wait(dve, L.has, 3 * (t.n - 1))
                v.tensor_scalar(ota[:, t.slot2, :], tyr[:, t.slot2, :], col[:, 0:1], None, ALU.is_equal)
                v.tensor_scalar(otb[:, t.slot2, :], tyr[:, t.slot2, :], col[:, 1:2], None, ALU.is_equal)
                v.tensor_scalar(selT[:, t.slot2, :], plr[:, t.slot2, :], col[:, 0:1], None, ALU.is_equal).then_inc(L.oh, 1)

            def split_scores(t):
                if t is None:
                    return
                steps = Steps(dve, L1.split, 3 * t.n)
                sn = cs[:, t.slot2, :, D + 1]
                dve.wait_ge(L1.cs, NBLK * (t.n + 1))
                steps.then(v.tensor_copy(sn3[:, :, 0], sn))
                steps.then(v.tensor_tensor(snr[:, 0, :], sn, sn3[:, :, 0], ALU.subtract))
                steps.then(v.tensor_copy(sn3[:, :, 1], snr[:, 0, :]))
                v.tensor_tensor(sn3[:, :, 2], snr[:, 0, :], sn3[:, :, 1], ALU.subtract).then_inc(L1.sn3, 1)

            mF, mB, d, w, sF, sB, rc, al = (rows[0:GS, c, :] for c in range(8))

            def scores(m, steps):
                L = L1
                sd, b0, b = sc[:, 0, :], sc[:, 1, :], sc[:, 2, :]
                dve.wait_ge(L.sd, m.n + 1)
                dve.wait_ge(L.cs, NBLK * (m.n + 1))
                steps.then(v.tensor_reduce(sd, sd_p.rearrange("p (g a) -> p g a", a=3), AX, ALU.add))
                steps.then(v.tensor_tensor(b0, sd, cs[:, m.slot2, :, D], ALU.add))
                v.scalar_tensor_tensor(b, b0, SLOPE, b0, ALU.mult, ALU.max).then_inc(L.b, 1)

            def maxima(m, steps):
                dve.wait_ge(L1.rows_in[m.slot4], 32 * (m.round4 + 1))
                dve.wait_ge(L1.bT, m.n + 1)
                reset = scn[:, m.slot4, :, :]
                steps.then(v.tensor_tensor_scan(mF, reset[:, 0, :], bT_p, -FAR, ALU.add, ALU.max))
                steps.then(v.tensor_tensor_scan(mB[:, ::-1], reset[:, 1, ::-1], mF[:, ::-1], -FAR, ALU.add, ALU.max))
                v.tensor_tensor(d, bT_p, mB, ALU.subtract).then_inc(L1.d, 1)

            def weights(m, steps):
                dve.wait_ge(L1.w, m.n + 1)
                reset = scn[:, m.slot4, :, :]
                steps.then(v.tensor_tensor_scan(sF, reset[:, 2, :], w, 0.0, ALU.mult, ALU.add))
                steps.then(v.tensor_tensor_scan(sB[:, ::-1], reset[:, 3, ::-1], sF[:, ::-1], 0.0, ALU.mult, ALU.max))
                steps.then(v.reciprocal(rc, sB))
                v.tensor_tensor(al, w, rc, ALU.mult).then_inc(L1.al, 1)

            def select(L, m, q):
                if q >= 2:
                    dve.wait_ge(L.y, NBLK * m.n + q - 1)
                for j in range(BG):
                    g = q * BG + j
                    if L is L1:
                        last = v.tensor_scalar(sel[:, q % 2, j, :], row[:, :], plc[:, m.slot4, g:g + 1],
                                               alpha[:, 0, g:g + 1], ALU.is_equal, ALU.mult)
                    else:
                        last = v.tensor_scalar(sel[:, q % 2, j, :], row[:, :], plc[:, m.slot4, g:g + 1], None,
                                               ALU.is_equal)
                last.then_inc(L.sel, 1)

            def add1(m, f, steps):
                L = L1
                dve.wait_ge(L.qc, NBLK * m.n + f + 1)
                if f == 1:
                    wait(dve, L.x1, m.n)
                elif f >= 2:
                    dve.wait_ge(L.second, steps.done + SOFT + f - 1)
                v.tensor_tensor(lr[:, f % 2, :], y_p[:, f % 2, :], qc[:, f % 2, :], ALU.max).then_inc(L.yfree, 1)
                dve.wait_ge(L.yfree, 2 + NBLK * m.n + f + 1)
                xs = xn[:, m.slot4, f * BG:(f + 1) * BG, :].rearrange("p a b -> p (a b)")
                last = v.tensor_tensor(xs, xs, lr[:, f % 2, :], ALU.add)
                if f < NBLK - 1:
                    steps.mark(last)
                else:
                    last.then_inc(L.x1, 1)

            def turn1(n, t, m):
                L = L1
                if m is None:
                    one_hots(n)
                    for part in range(8):
                        stats_some(L, n, part)
                    variances(L, 1, n)
                    factors(L, 1, n)
                    split_scores(t)
                    return
                steps = Steps(dve, L.second, K_SECOND * m.n)
                scores(m, steps)
                stats_some(L, n, 0)
                maxima(m, steps)
                stats_some(L, n, 1)
                weights(m, steps)
                one_hots(n)
                dve.wait_ge(L.alT, m.n + 1)
                steps.then(v.tensor_copy(alpha[:, 0, :], alT_p))
                select(L, m, 0)
                select(L, m, 1)
                stats_some(L, n, 2)
                add1(m, 0, steps)
                select(L, m, 2)
                stats_some(L, n, 3)
                stats_some(L, n, 4)
                add1(m, 1, steps)
                select(L, m, 3)
                for part in range(5, 8):
                    stats_some(L, n, part)
                variances(L, 1, n)
                add1(m, 2, steps)
                factors(L, 1, n)
                split_scores(t)
                add1(m, 3, steps)
                assert steps.n == K_SECOND, steps.n

            def own_row(m, q):
                dve.wait_ge(L2.an, NBLK * m.n + q + 1)
                xs = xn[:, m.slot4, q * BG:(q + 1) * BG, :]
                v.tensor_tensor(xs, xs, own[:, m.slot2, q * BG:(q + 1) * BG, :], ALU.add).then_inc(L2.second, 1)

            def add2(m, f):
                dve.wait_ge(L2.second, NBLK * m.n + f + 1)
                dve.wait_ge(L2.y, NBLK * m.n + f + 1)
                xs = xn[:, m.slot4, f * BG:(f + 1) * BG, :].rearrange("p a b -> p (a b)")
                v.tensor_tensor(xs, xs, y_p[:, f % 2, :], ALU.add).then_inc(L2.yfree, 1)

            def turn2(n, t, m):
                L = L2
                if m is None:
                    for part in range(8):
                        stats_some(L, n, part)
                    variances(L, 2, n)
                    factors(L, 2, n)
                    return
                dve.wait_ge(L.rows_in[m.slot4], 16 * (m.round4 + 1))
                select(L, m, 0)
                select(L, m, 1)
                for q in range(NBLK):
                    own_row(m, q)
                    stats_some(L, n, 2 * q)
                    if q >= 2:
                        select(L, m, q)
                    if q > 0:
                        add2(m, q - 1)
                    stats_some(L, n, 2 * q + 1)
                variances(L, 2, n)
                add2(m, NBLK - 1)
                factors(L, 2, n)

            dve.wait_ge(k_free, NK + 1)
            v.memset(alpha[:, 1, 0:1], 0.0).then_inc(L1.yfree, 2)
            v.memset(alpha[:, 1, 1:2], 0.0).then_inc(L2.yfree, 2)
            run(v.Fori, turn1)
            dve.wait_ge(L1.second, K_SECOND * NSB)
            run(v.Fori, turn2)

        @block.scalar
        def _(act):
            a = nc.scalar.activation

            def inverse_roots(L, t):
                if t is None:
                    return
                act.wait_ge(L.var, t.n + 1)
                a(lnv[:, :], var[:, :], ACT.Ln).then_inc(L.ln, 1)
                act.wait_ge(L.ln, t.n + 1)
                a(rstd0[:, :], lnv[:, :], ACT.Exp, scale=-0.5).then_inc(L.rstd0, 1)

            def norm(L, t, q, function, to, rows_, base, signal):
                for j in range(BG):
                    g = q * BG + j
                    last = a(to[:, j, :], rows_[:, g, :], function, bias=nbias[:, t.slot2, base + g:base + g + 1],
                             scale=rstd[:, t.slot2, base + g:base + g + 1])
                last.then_inc(signal, 1)

            def exponentials(m):
                act.wait_ge(L1.d, m.n + 1)
                a(rows[0:GS, 3, :], rows[0:GS, 2, :], ACT.Exp).then_inc(L1.w, 1)

            def messages_out(t, q):
                act.wait_ge(L1.c, NBLK * t.n + q + 1)
                if q == 0:
                    wait(act, L1.y, NBLK * (t.n - 1))
                a(cs[:, t.slot2, q * BG:(q + 1) * BG, :].rearrange("p (a b) c -> p a (b c)", a=2),
                  c_p[:, :, 0:2 * (D + 2)], ACT.Copy).then_inc(L1.cs, 1)

            def slopes(m, q):
                act.wait_ge(L1.y, NBLK * m.n + q + 1)
                act.wait_ge(L1.yfree, NBLK * m.n + q + 1)
                a(qc[:, q % 2, :], y_p[:, q % 2, :], ACT.Copy, scale=SLOPE).then_inc(L1.qc, 1)

            def normed(t, q):
                if t is None:
                    return
                L = L1
                if q == 0:
                    act.wait_ge(L.rstd, t.n + 1)
                wait(act, L.tn, NBLK * t.n + q - 1)
                norm(L, t, q, ACT.Identity, an[:, q % 2, :, :], xn[:, t.slot4, :, :], GS, L.an)
                wait(act, L.te, NBLK * t.n + q - 1)
                norm(L, t, q, ACT.Identity, ae[:, q % 2, :, :], xe[:, t.slot4, :, :], 0, L.ae)

            def turn1(n, t, m):
                L = L1
                if t is None and m is not None:
                    exponentials(m)
                for q in range(NBLK):
                    if t is not None:
                        act.wait_ge(L.tn, NBLK * t.n + q + 1)
                        wait(act, L.y, NBLK * (t.n - 1))
                        a(hnT[:, t.slot2, q * BG * P:(q + 1) * BG * P], tn_p[:, :], ACT.Relu).then_inc(L.hn, 1)
                        act.wait_ge(L.te, NBLK * t.n + q + 1)
                        wait(act, L.c, NBLK * t.n + q - 1)
                        a(heT[:, q % 2, :], te_p[:, q % 2, :], ACT.Relu).then_inc(L.he, 1)
                        if q == 0 and m is not None:
                            exponentials(m)
                    if q > 0 and m is not None:
                        slopes(m, q - 1)
                    if t is not None and q < NBLK - 1:
                        normed(t, q + 1)
                    if q == NBLK - 1:
                        inverse_roots(L, n)
                    if t is not None:
                        messages_out(t, q)
                if m is not None:
                    slopes(m, NBLK - 1)
                normed(n, 0)

            def turn2(n, t, m):
                L = L2
                if t is not None:
                    act.wait_ge(L.rstd, t.n + 1)
                    wait(act, L.y, NBLK * (t.n - 1))
                    wait(act, L.second, NBLK * (t.n - 1))
                    for q in range(NBLK):
                        norm(L, t, q, ACT.Relu, own[:, t.slot2, q * BG:(q + 1) * BG, :], xn[:, t.slot4, :, :], GS, L.an)
                        norm(L, t, q, ACT.Relu, h2[:, t.slot2, q * BG:(q + 1) * BG, :], xe[:, t.slot4, :, :], 0, L.ae)
                inverse_roots(L, n)

            nc.scalar.preload_act_table_set("natural_log_exp_and_others")
            run(nc.scalar.Fori, turn1)
            run(nc.scalar.Fori, turn2)

        @block.tensor
        def _(pe):
            mm, tr = nc.tensor.matmul, nc.tensor.transpose

            def messages(t, q):
                L = L1
                pe.wait_ge(L.he, NBLK * t.n + q + 1)
                pe.wait_ge(L.hn, NBLK * t.n + q + 1)
                pe.wait_ge(L.oh, t.n + 1)
                wait(pe, L.cs, NBLK * t.n + q)
                for j in range(BG):
                    s = slice((q * BG + j) * P, (q * BG + j + 1) * P)
                    at = j % 2 * (D + 2)
                    to = c_p[:, j // 2, at:at + D + 1]
                    mm(to, heT[:, q % 2, j * P:(j + 1) * P], w1a[:, :], start=True, stop=False)
                    for part in range(3):
                        mm(to, ota[:, t.slot2, s], rel3[:, 0, part, :], start=False, stop=False)
                    for part in range(3):
                        mm(to, otb[0:RB, t.slot2, s], rel3[0:RB, 1, part, :], start=False, stop=part == 2)
                    last = mm(c_p[:, j // 2, at + D + 1:at + D + 2], hnT[:, t.slot2, s], ub[:, :], start=True, stop=True)
                last.then_inc(L.c, 1)

            def aggregate1(m, q):
                L = L1
                pe.wait_ge(L.sel, NBLK * m.n + q + 1)
                pe.wait_ge(L.yfree, NBLK * m.n + q + 1)
                for j in range(BG):
                    g = q * BG + j
                    to = y_p[:, q % 2, j * D:(j + 1) * D]
                    mm(to, hnT[:, m.slot2, g * P:(g + 1) * P], w1s[:, 1, :], start=True, stop=False)
                    last = mm(to, sel[:, q % 2, j, :], cs[:, m.slot2, g, 0:D], start=False, stop=True)
                last.then_inc(L.y, 1)

            def scores_to_rows(m):
                pe.wait_ge(L1.b, m.n + 1)
                tr(bT_p, sc[:, 2, :], ident[:, :]).then_inc(L1.bT, 1)

            def weights_to_columns(m):
                pe.wait_ge(L1.al, m.n + 1)
                mm(alT_p, rows[:, 7, :], ident[:, 0:GS], start=True, stop=True).then_inc(L1.alT, 1)

            def destination_scores(t):
                L = L1
                pe.wait_ge(L.sn3, t.n + 1)
                wait(pe, L.b, t.n)
                for g in range(GS):
                    last = mm(sd_p[:, 3 * g:3 * g + 3], selT[:, t.slot2, g * P:(g + 1) * P], sn3[:, g, :], start=True, stop=True)
                last.then_inc(L.sd, 1)

            def nodes_turned(t, q):
                pe.wait_ge(L1.an, NBLK * t.n + q + 1)
                wait(pe, L1.hn, NBLK * t.n + q)
                for j in range(BG):
                    last = tr(tn_p[:, j * P:(j + 1) * P], an[:, q % 2, j, :], ident[:, :])
                last.then_inc(L1.tn, 1)

            def edges_turned(t, q):
                pe.wait_ge(L1.ae, NBLK * t.n + q + 1)
                wait(pe, L1.he, NBLK * t.n + q - 1)
                for j in range(BG):
                    last = tr(te_p[:, q % 2, j * P:(j + 1) * P], ae[:, q % 2, j, :], ident[:, :])
                last.then_inc(L1.te, 1)

            def turn1(n, t, m):
                if m is not None:
                    scores_to_rows(m)
                if t is None and m is not None:
                    weights_to_columns(m)
                for q in range(NBLK):
                    if t is not None:
                        messages(t, q)
                        if q == 0 and m is not None:
                            weights_to_columns(m)
                        if q < NBLK - 1:
                            nodes_turned(t, q + 1)
                            edges_turned(t, q + 1)
                    if m is not None:
                        aggregate1(m, q)
                if t is not None:
                    destination_scores(t)
                if n is not None:
                    nodes_turned(n, 0)
                    edges_turned(n, 0)

            def turn2(n, t, m):
                L = L2
                if m is None:
                    return
                for q in range(NBLK):
                    pe.wait_ge(L.ae, NBLK * m.n + q + 1)
                    pe.wait_ge(L.sel, NBLK * m.n + q + 1)
                    pe.wait_ge(L.yfree, NBLK * m.n + q + 1)
                    for j in range(BG):
                        last = mm(y_p[:, q % 2, j * D:(j + 1) * D], sel[:, q % 2, j, :], h2[:, m.slot2, q * BG + j, :],
                                  start=True, stop=True)
                    last.then_inc(L.y, 1)

            run(nc.tensor.Fori, turn1)
            run(nc.tensor.Fori, turn2)


def kernel(x, src, dst, edge_type_200, L0_gnn_relation_embedding, L0_gnn_W1, L0_gnn_b1, L0_gnn_w2):
    import numpy as np
    import concourse.bacc as bacc
    from concourse.bass_utils import run_bass_kernel_spmd

    nc = bacc.Bacc("TRN2", target_bir_lowering=False, num_devices=1)
    n_edges, n_nodes = src.shape[0], x.shape[0]
    width = -(-(n_edges + P) // (4 * P)) * 4 * P

    def padded(a, end):
        return np.concatenate([a, np.full(width - n_edges, end, a.dtype)]).reshape(1, width)

    arrays = {"x": np.ascontiguousarray(x), "src": padded(src, 0), "dst": padded(dst, 2 * n_nodes),
              "typ": padded(edge_type_200, 0), "rel": np.ascontiguousarray(L0_gnn_relation_embedding),
              "w1": np.ascontiguousarray(L0_gnn_W1), "b1": np.ascontiguousarray(L0_gnn_b1), "w2": np.ascontiguousarray(L0_gnn_w2)}
    args = [nc.dram_tensor(f"in_{k}", a.shape, mybir.dt.from_np(a.dtype), kind="ExternalInput").ap() for k, a in arrays.items()]
    out = nc.dram_tensor("out", x.shape, mybir.dt.float32, kind="ExternalOutput").ap()
    gnn_two_layers(nc, *args, out)
    r = run_bass_kernel_spmd(nc, [{f"in_{k}": a for k, a in arrays.items()}], core_ids=[0])
    return r.results[0]["out"]
```

```python
import concourse.bass as bass
from concourse import mybir
from contextlib import ExitStack

P = 128
D = 128
GS = 16
BG = 4
NBLK = GS // BG
EPS = 1e-5
SLOPE = 0.01
FAR = float(2.0 ** 100)
SKIP = float(2 ** 20)
OFF = 200.0


def wait(engine, semaphore, value):
    if isinstance(value, int) and value <= 0:
        return
    engine.wait_ge(semaphore, value)


class At:

    def __init__(self, i, k):
        self.n = 4 * i + k
        self.slot4, self.round4 = k % 4, i + k // 4
        self.slot2, self.round2 = k % 2, 2 * i + k // 2


class Semaphores:

    def __init__(self, sem, n):
        def several(name, count):
            return [sem(f"{name}{s}_{n}") for s in range(count)]

        self.x_in = several("x_in", 4)
        self.rest_in = sem(f"rest_in_{n}")
        self.idx_in = several("idx_in", 4)
        self.rows_in = several("rows_in", 4)
        self.gathered = several("gathered", 4)
        self.stored = several("stored", 4)
        self.turns = sem(f"turns_{n}")
        self.row_turns = sem(f"row_turns_{n}")
        self.var = sem(f"var_{n}")
        self.ln = sem(f"ln_{n}")
        self.rstd0 = sem(f"rstd0_{n}")
        self.rstd = sem(f"rstd_{n}")
        self.ae = sem(f"ae_{n}")
        self.an = sem(f"an_{n}")
        self.sel = sem(f"sel_{n}")
        self.y = sem(f"y_{n}")
        self.yfree = sem(f"yfree_{n}")
        self.x1 = sem(f"x1_{n}")
        self.first = sem(f"first_{n}")
        self.second = sem(f"second_{n}")
        if n == 2:
            return
        self.tables_in = several("tables_in", 2)
        self.tn = sem("tn")
        self.te = sem("te")
        self.hn = sem("hn")
        self.he = sem("he")
        self.oh = sem("oh")
        self.c = sem("c")
        self.cs = sem("cs")
        self.split = sem("split")
        self.sn3 = sem("sn3")
        self.sd = sem("sd")
        self.b = sem("b")
        self.bT = sem("bT")
        self.d = sem("d")
        self.w = sem("w")
        self.al = sem("al")
        self.alT = sem("alT")
        self.qc = sem("qc")
        self.has_turns = sem("has_turns")
        self.has = sem("has")


class Steps:

    def __init__(self, engine, semaphore, done):
        self.engine, self.semaphore, self.done = engine, semaphore, done
        self.n = 0

    def mark(self, instruction):
        self.n += 1
        instruction.then_inc(self.semaphore, 1)

    def settle(self):
        self.engine.wait_ge(self.semaphore, self.done + self.n)

    def then(self, instruction):
        self.mark(instruction)
        self.settle()


def general_path(nc, ctx, sem, buffers, x, src_e, dst_e, typ_e, out):
    f32, i32, u32 = mybir.dt.float32, mybir.dt.int32, mybir.dt.uint32
    ALU, ACT, AX = mybir.AluOpType, mybir.ActivationFunctionType, mybir.AxisListType.X
    ident, w1a, w1s, ub, relw, R, te_p, c_p, y_p, xe, ae, sel, rows, tiny = buffers
    N, T = x.shape[0], dst_e.shape[1] // P
    NP = -(-N // (GS * P)) * GS * P
    C = D + 1
    full, rest = N // P, N % P

    def table(name, n, m):
        return nc.dram_tensor(name, (n, m), f32, kind="Internal").ap()

    relw_d, c_d = table("relw_d", R, C), table("c_d", T * P, C)
    max_d, sum_d, agg_d, mid_d = table("max_d", NP, 1), table("sum_d", NP, C), table("agg_d", NP, C), table("mid_d", N, D)

    def flat(a, n):
        return a.rearrange("p a b -> p (a b)")[:, 0:n]

    w1b = flat(xe[:, 0, 0:2, :], C)
    cb, gathered, joined, ha = (flat(xe[:, 0, 2 * k:2 * k + 2, :], C) for k in (1, 2, 3, 4))
    zeros = flat(xe[:, 1, :, :], 7 * C)
    ones_row = xe[:, 2, 0, :]
    x_src, x_dst, h_src, h_dst = (ae[:, 0, k, :] for k in range(4))
    hT = flat(ae[:, 1, 0:2, :], 2 * P)
    same, mask, masked = (sel[:, 0, k, :] for k in range(3))
    small = rows[:, 0, :]
    dst_f, top, best, shift, weight, inverse, other, best0, log_var, root0 = (small[:, k:k + 1] for k in range(10))
    v = nc.vector
    src_i, dst_i, typ_i = (rows[:, 1, k:k + 1].bitcast(i32) for k in range(3))

    started = sem("g_started")
    turned = sem("g_turned")

    class Chain:

        def __init__(self, dve, semaphore, turn, per):
            self.dve, self.semaphore, self.base, self.n = dve, semaphore, turn * per, 0

        def then(self, instruction):
            self.n += 1
            instruction.then_inc(self.semaphore, 1)
            self.dve.wait_ge(self.semaphore, self.base + self.n)

    class Roots:

        def __init__(self, name, per):
            self.per = per
            self.var, self.ln, self.root = sem(name + "_var"), sem(name + "_ln"), sem(name + "_root")

        def scalar_turn(self, act, t):
            for k in range(self.per):
                act.wait_ge(self.var, self.per * t + k + 1)
                nc.scalar.activation(log_var, tiny[:, 1, 5:6], ACT.Ln).then_inc(self.ln, 1)
                act.wait_ge(self.ln, self.per * t + k + 1)
                nc.scalar.activation(root0, log_var, ACT.Exp, scale=-0.5).then_inc(self.root, 1)

    def norm_relu(chain, into, rows_, roots, t, k):
        st, mv = tiny[:, 0, 0:6], tiny[:, 1, 0:6]
        chain.then(v.bn_stats(st, rows_))
        v.tensor_tensor(mv[:, 0:1], st[:, 1:2], st[:, 4:5], ALU.add)
        v.tensor_tensor(mv[:, 1:2], st[:, 1:2], st[:, 4:5], ALU.subtract)
        chain.then(v.tensor_tensor(mv[:, 2:3], st[:, 2:3], st[:, 5:6], ALU.add))
        v.tensor_scalar(mv[:, 0:1], mv[:, 0:1], 0.5, None, ALU.mult)
        v.scalar_tensor_tensor(mv[:, 3:4], mv[:, 1:2], 0.25, mv[:, 1:2], ALU.mult, ALU.mult)
        chain.then(v.tensor_scalar(mv[:, 4:5], mv[:, 2:3], 1.0 / D, EPS, ALU.mult, ALU.add))
        v.tensor_tensor(mv[:, 5:6], mv[:, 3:4], mv[:, 4:5], ALU.add).then_inc(roots.var, 1)
        chain.dve.wait_ge(roots.root, roots.per * t + k + 1)
        chain.then(v.tensor_copy(st[:, 0:1], root0))
        chain.then(v.scalar_tensor_tensor(st[:, 1:2], mv[:, 5:6], -0.5, st[:, 0:1], ALU.mult, ALU.mult))
        chain.then(v.tensor_tensor(st[:, 2:3], st[:, 1:2], st[:, 0:1], ALU.mult))
        chain.then(v.scalar_tensor_tensor(st[:, 3:4], st[:, 2:3], 1.5, st[:, 0:1], ALU.add, ALU.mult))
        chain.then(v.tensor_scalar(into, rows_, mv[:, 0:1], st[:, 3:4], ALU.subtract, ALU.mult))
        chain.then(v.tensor_scalar(into, into, 0.0, None, ALU.max))

    NORM = 9

    def tile_of(e, t):
        return e[:, bass.ds(t * P, P)].rearrange("o (p c) -> (o p) c", p=P)

    def rows_of(a, t, n=P):
        return a[bass.ds(t * P, n), :]

    def gather(into, a, at, n, moved):
        nc.gpsimd.indirect_dma_start(out=into, out_offset=None, in_=a,
                                     in_offset=bass.IndirectOffsetOnAxis(ap=at.bitcast(u32), axis=0),
                                     bounds_check=n, oob_is_err=False).then_inc(moved, 16)

    def scatter(a, at, from_, n, moved):
        nc.gpsimd.indirect_dma_start(out=a, out_offset=bass.IndirectOffsetOnAxis(ap=at.bitcast(u32), axis=0), in_=from_,
                                     in_offset=None, bounds_check=n, oob_is_err=False).then_inc(moved, 16)

    with nc.Block() as block:
        ready = sem("g_ready")

        @block.vector
        def _(dve):
            v.memset(zeros, 0.0)
            v.memset(ones_row, -FAR)
            v.memset(cb, 0.0)
            v.memset(gathered, 0.0)
            v.memset(ha, 1.0)
            for k in range(2):
                v.memset(ae[:, k, :, :], 0.0)
            v.memset(rows[:, 0, :], 0.0)
            v.tensor_copy(w1b[:, 0:D], w1s[:, 1, :])
            v.tensor_copy(w1b[:, D:C], ub[:, :]).then_inc(ready, 1)

        @block.sync
        def _(sp):
            sp.wait_ge(ready, 1)
            sp.dma_start(relw_d[0:P, :], relw[:, 0, :]).then_inc(started, 16)
            sp.dma_start(relw_d[P:R, :], relw[0:R - P, 1, :]).then_inc(started, 16)
            with nc.sync.Fori(0, NP // (GS * P)) as t:
                sp.dma_start(max_d[bass.ds(t * GS * P, GS * P), :].rearrange("(p c) o -> p (c o)", p=P), ones_row[:, 0:GS]
                             ).then_inc(started, 16)
                for half in range(GS):
                    for a in (sum_d, agg_d):
                        sp.dma_start(a[bass.ds(t * GS * P + half * P, P), :], zeros[:, 0:C]).then_inc(started, 16)
            sp.wait_ge(started, 32 + NP // (GS * P) * 16 * (1 + 2 * GS))

    with nc.Block() as block:
        walk, inner, moved = sem("g_messages"), sem("g_messages_dve"), sem("g_messages_moved")
        K, KD = 151, 2 * NORM + 8
        roots = Roots("g_messages", 2)

        @block.sync
        def _(sp):
            sp.sem_inc(walk, 1)
            with nc.sync.Fori(0, T) as t:
                sp.wait_ge(walk, K * t + 1)
                for i, e in ((src_i, src_e), (dst_i, dst_e), (typ_i, typ_e)):
                    sp.dma_start(i, tile_of(e, t)).then_inc(walk, 16)
                sp.wait_ge(walk, K * t + 120)
                sp.dma_start(rows_of(c_d, t), cb).then_inc(walk, 16)
            sp.wait_ge(walk, K * T + 1)

        @block.gpsimd
        def _(pool):
            last_row, last_rel = nc.gpsimd.to_reg(N - 1), nc.gpsimd.to_reg(R - 1)
            with nc.gpsimd.Fori(0, T) as t:
                pool.wait_ge(walk, K * t + 49)
                pool.sem_inc(turned, 1)
                gather(x_src, x, src_i, last_row, moved)
                gather(x_dst, x, dst_i, last_row, moved)
                gather(gathered, relw_d, typ_i, last_rel, moved)
                gather(best0, max_d, dst_i, last_row, moved)
                pool.wait_ge(moved, 80 * t + 64)
                pool.sem_inc(walk, 64)
                pool.wait_ge(walk, K * t + 120)
                pool.sem_inc(turned, 1)
                scatter(max_d, dst_i, best, last_row, moved)
                pool.wait_ge(moved, 80 * t + 80)
                pool.sem_inc(walk, 16)

        @block.vector
        def _(dve):
            with nc.vector.Fori(0, T) as t:
                chain = Chain(dve, inner, t, KD)
                dve.wait_ge(walk, K * t + 113)
                chain.then(v.tensor_copy(dst_f, dst_i))
                norm_relu(chain, h_src, x_src, roots, t, 0)
                norm_relu(chain, h_dst, x_dst, roots, t, 1)
                v.memset(other, 0.0).then_inc(walk, 1)
                dve.wait_ge(walk, K * t + 115)
                chain.then(v.tensor_copy(hT, te_p[:, 0, 0:2 * P]))
                chain.then(v.tensor_scalar(same, c_p[:, 0, 0:P], dst_f, None, ALU.is_equal))
                v.tensor_scalar(mask, same, 1.0, FAR, ALU.subtract, ALU.mult).then_inc(walk, 1)
                dve.wait_ge(walk, K * t + 117)
                chain.then(v.tensor_tensor(cb, y_p[:, 0, 0:C], gathered, ALU.add))
                chain.then(v.tensor_scalar(other, cb[:, D:C], SLOPE, None, ALU.mult))
                v.tensor_tensor(cb[:, D:C], cb[:, D:C], other, ALU.max).then_inc(walk, 1)
                dve.wait_ge(walk, K * t + 119)
                chain.then(v.tensor_tensor(masked, c_p[:, 1, 0:P], mask, ALU.add))
                chain.then(v.tensor_reduce(top, masked, AX, ALU.max))
                chain.then(v.tensor_tensor(best, top, best0, ALU.max))
                assert chain.n == KD, chain.n
                v.memset(shift, 0.0).then_inc(walk, 1)

        @block.tensor
        def _(pe):
            with nc.tensor.Fori(0, T) as t:
                pe.wait_ge(walk, K * t + 114)
                nc.tensor.transpose(te_p[:, 0, 0:P], h_src, ident[:, :])
                nc.tensor.transpose(te_p[:, 0, P:2 * P], h_dst, ident[:, :])
                nc.tensor.transpose(c_p[:, 0, 0:P], dst_f.to_broadcast([P, P]), ident[:, :]).then_inc(walk, 1)
                pe.wait_ge(walk, K * t + 116)
                nc.tensor.matmul(y_p[:, 0, 0:C], hT[:, 0:P], w1a[:, :], start=True, stop=False)
                nc.tensor.matmul(y_p[:, 0, 0:C], hT[:, P:2 * P], w1b, start=False, stop=True).then_inc(walk, 1)
                pe.wait_ge(walk, K * t + 118)
                nc.tensor.transpose(c_p[:, 1, 0:P], cb[:, D:C].to_broadcast([P, P]), ident[:, :]).then_inc(walk, 1)

        @block.scalar
        def _(act):
            nc.scalar.preload_act_table_set("natural_log_exp_and_others")
            with nc.scalar.Fori(0, T) as t:
                roots.scalar_turn(act, t)

    with nc.Block() as block:
        walk, inner, moved = sem("g_sums"), sem("g_sums_dve"), sem("g_sums_moved")
        KS, KSD = 86, 5

        @block.sync
        def _(sp):
            sp.sem_inc(walk, 1)
            with nc.sync.Fori(0, T) as t:
                sp.wait_ge(walk, KS * t + 1)
                sp.dma_start(dst_i, tile_of(dst_e, t)).then_inc(walk, 16)
                sp.dma_start(cb, rows_of(c_d, t)).then_inc(walk, 16)
            sp.wait_ge(walk, KS * T + 1)

        @block.gpsimd
        def _(pool):
            last_row = nc.gpsimd.to_reg(N - 1)
            with nc.gpsimd.Fori(0, T) as t:
                pool.wait_ge(walk, KS * t + 33)
                pool.sem_inc(turned, 1)
                gather(best0, max_d, dst_i, last_row, moved)
                gather(gathered, sum_d, dst_i, last_row, moved)
                pool.wait_ge(moved, 48 * t + 32)
                pool.sem_inc(walk, 32)
                pool.wait_ge(walk, KS * t + 71)
                pool.sem_inc(turned, 1)
                scatter(sum_d, dst_i, joined, last_row, moved)
                pool.wait_ge(moved, 48 * t + 48)
                pool.sem_inc(walk, 16)

        @block.vector
        def _(dve):
            with nc.vector.Fori(0, T) as t:
                chain = Chain(dve, inner, t, KSD)
                dve.wait_ge(walk, KS * t + 65)
                chain.then(v.tensor_copy(dst_f, dst_i))
                chain.then(v.tensor_tensor(other, cb[:, D:C], best0, ALU.subtract))
                v.tensor_scalar(shift, other, 0.0, None, ALU.min).then_inc(walk, 1)
                dve.wait_ge(walk, KS * t + 68)
                chain.then(v.tensor_scalar(same, c_p[:, 0, 0:P], dst_f, None, ALU.is_equal))
                chain.then(v.memset(cb[:, D:C], 1.0))
                v.tensor_scalar(cb, cb, weight, None, ALU.mult).then_inc(walk, 1)
                dve.wait_ge(walk, KS * t + 70)
                chain.then(v.tensor_tensor(joined, y_p[:, 0, 0:C], gathered, ALU.add))
                assert chain.n == KSD, chain.n
                v.memset(other, 0.0).then_inc(walk, 1)

        @block.scalar
        def _(act):
            nc.scalar.preload_act_table_set("natural_log_exp_and_others")
            with nc.scalar.Fori(0, T) as t:
                act.wait_ge(walk, KS * t + 66)
                nc.scalar.activation(weight, shift, ACT.Exp).then_inc(walk, 1)

        @block.tensor
        def _(pe):
            with nc.tensor.Fori(0, T) as t:
                pe.wait_ge(walk, KS * t + 67)
                nc.tensor.transpose(c_p[:, 0, 0:P], dst_f.to_broadcast([P, P]), ident[:, :]).then_inc(walk, 1)
                pe.wait_ge(walk, KS * t + 69)
                nc.tensor.matmul(y_p[:, 0, 0:C], same, cb, start=True, stop=True).then_inc(walk, 1)

    def dense(name, a, sums, to, per, roots, arithmetic):
        walk, inner = sem(name), sem(name + "_dve")
        with nc.Block() as block:

            @block.sync
            def _(sp):
                def tile(t, n):
                    sp.wait_ge(walk, 49 * t + 1)
                    sp.dma_start(x_src[0:n, :], rows_of(a, t, n)).then_inc(walk, 16)
                    sp.dma_start(gathered[0:n, :], rows_of(sums, t, n)).then_inc(walk, 16)
                    sp.wait_ge(walk, 49 * t + 34)
                    sp.dma_start(rows_of(to, t, n), x_dst[0:n, :]).then_inc(walk, 16)

                sp.sem_inc(walk, 1)
                with nc.sync.Fori(0, full) as t:
                    tile(t, P)
                if rest:
                    tile(full, rest)
                sp.wait_ge(walk, 49 * (full + (rest > 0)) + 1)

            @block.vector
            def _(dve):
                def tile(t):
                    dve.wait_ge(walk, 49 * t + 33)
                    chain = Chain(dve, inner, t, per)
                    arithmetic(chain, roots, t)
                    assert chain.n == per, chain.n
                    v.memset(shift, 0.0).then_inc(walk, 1)

                with nc.vector.Fori(0, full) as t:
                    tile(t)
                if rest:
                    tile(full)

            @block.scalar
            def _(act):
                if roots is None:
                    return
                nc.scalar.preload_act_table_set("natural_log_exp_and_others")
                with nc.scalar.Fori(0, full) as t:
                    roots.scalar_turn(act, t)
                if rest:
                    roots.scalar_turn(act, full)

    def first_layer(chain, roots, t):
        chain.then(v.tensor_scalar(other, gathered[:, D:C], 0.5, None, ALU.max))
        chain.then(v.reciprocal(inverse, other))
        chain.then(v.tensor_scalar(h_src, gathered[:, 0:D], inverse, None, ALU.mult))
        chain.then(v.scalar_tensor_tensor(h_dst, h_src, SLOPE, h_src, ALU.mult, ALU.max))
        chain.then(v.tensor_tensor(x_dst, x_src, h_dst, ALU.add))

    dense("g_first", x, sum_d, mid_d, 5, None, first_layer)

    with nc.Block() as block:
        walk, inner, moved = sem("g_agg"), sem("g_agg_dve"), sem("g_agg_moved")
        KG, KGD = 85, NORM + 3
        roots = Roots("g_agg", 1)

        @block.sync
        def _(sp):
            sp.sem_inc(walk, 1)
            with nc.sync.Fori(0, T) as t:
                sp.wait_ge(walk, KG * t + 1)
                sp.dma_start(src_i, tile_of(src_e, t)).then_inc(walk, 16)
                sp.dma_start(dst_i, tile_of(dst_e, t)).then_inc(walk, 16)
            sp.wait_ge(walk, KG * T + 1)

        @block.gpsimd
        def _(pool):
            last_row = nc.gpsimd.to_reg(N - 1)
            with nc.gpsimd.Fori(0, T) as t:
                pool.wait_ge(walk, KG * t + 33)
                pool.sem_inc(turned, 1)
                gather(x_src, mid_d, src_i, last_row, moved)
                gather(gathered, agg_d, dst_i, last_row, moved)
                pool.wait_ge(moved, 48 * t + 32)
                pool.sem_inc(walk, 32)
                pool.wait_ge(walk, KG * t + 70)
                pool.sem_inc(turned, 1)
                scatter(agg_d, dst_i, joined, last_row, moved)
                pool.wait_ge(moved, 48 * t + 48)
                pool.sem_inc(walk, 16)

        @block.vector
        def _(dve):
            with nc.vector.Fori(0, T) as t:
                chain = Chain(dve, inner, t, KGD)
                dve.wait_ge(walk, KG * t + 65)
                chain.then(v.tensor_copy(dst_f, dst_i))
                norm_relu(chain, ha[:, 0:D], x_src, roots, t, 0)
                v.memset(shift, 0.0).then_inc(walk, 1)
                dve.wait_ge(walk, KG * t + 67)
                chain.then(v.tensor_scalar(same, c_p[:, 0, 0:P], dst_f, None, ALU.is_equal))
                v.memset(shift, 0.0).then_inc(walk, 1)
                dve.wait_ge(walk, KG * t + 69)
                chain.then(v.tensor_tensor(joined, y_p[:, 0, 0:C], gathered, ALU.add))
                assert chain.n == KGD, chain.n
                v.memset(shift, 0.0).then_inc(walk, 1)

        @block.tensor
        def _(pe):
            with nc.tensor.Fori(0, T) as t:
                pe.wait_ge(walk, KG * t + 66)
                nc.tensor.transpose(c_p[:, 0, 0:P], dst_f.to_broadcast([P, P]), ident[:, :]).then_inc(walk, 1)
                pe.wait_ge(walk, KG * t + 68)
                nc.tensor.matmul(y_p[:, 0, 0:C], same, ha, start=True, stop=True).then_inc(walk, 1)

        @block.scalar
        def _(act):
            nc.scalar.preload_act_table_set("natural_log_exp_and_others")
            with nc.scalar.Fori(0, T) as t:
                roots.scalar_turn(act, t)

    def second_layer(chain, roots, t):
        norm_relu(chain, h_src, x_src, roots, t, 0)
        chain.then(v.tensor_scalar(other, gathered[:, D:C], 0.5, None, ALU.is_lt))
        chain.then(v.scalar_tensor_tensor(h_dst, h_src, other, gathered[:, 0:D], ALU.mult, ALU.add))
        chain.then(v.tensor_tensor(x_dst, x_src, h_dst, ALU.add))

    dense("g_second", mid_d, agg_d, out, NORM + 3, Roots("g_second", 1), second_layer)


def gnn_two_layers(nc, x, src_e, dst_e, typ_e, rel, w1, b1, w2, out):
    f32, bf16, i32, u32 = mybir.dt.float32, mybir.dt.bfloat16, mybir.dt.int32, mybir.dt.uint32
    ALU, ACT, AX = mybir.AluOpType, mybir.ActivationFunctionType, mybir.AxisListType.X

    N = x.shape[0]
    EC = dst_e.shape[1] // P
    R = rel.shape[0]
    RB = R - P
    NSB = -(-N // (GS * P))
    NG = NSB * GS
    NK = -(-NG // P)
    LOOPS = (NSB - 1) // 4
    assert NSB == 4 * LOOPS + 1 and EC % 4 == 0
    TAIL = N - (NSB - 1) * GS * P
    TG, TR = TAIL // P, TAIL % P
    assert TG > 1

    starts_d = nc.dram_tensor("starts_d", (1024, 1), i32, kind="Internal").ap()
    scan_d = nc.dram_tensor("scan_d", (NK * P, 4 * P), f32, kind="Internal").ap()
    place_d = nc.dram_tensor("place_d", (NK * P, P), bf16, kind="Internal").ap()
    types_d = nc.dram_tensor("types_d", (NK * P, P), bf16, kind="Internal").ap()
    x1_d = nc.dram_tensor("x1_d", (N, D), f32, kind="Internal").ap()

    ctx = ExitStack()
    with ctx:
        def sb(name, shape, dt):
            return ctx.enter_context(nc.sbuf_tensor(name, shape, dt))

        def pb(name, shape, dt):
            return ctx.enter_context(nc.psum_tensor(name, shape, dt))

        def sem(name):
            return ctx.enter_context(nc.semaphore(name))

        ident = sb("ident", [P, P], f32)
        row = sb("row", [P, P], f32)
        col = sb("col", [P, 2], f32)
        gbase = sb("gbase", [P, NK], f32)
        fold = sb("fold", [P, 32], f32)
        below = sb("below", [32, 32], f32)
        blocks4 = sb("blocks4", [P, 4], f32)
        row32 = sb("row32", [P, 32], f32)
        ones = sb("ones", [P, 1], f32)
        w1s = sb("w1s", [P, 3, D], f32)
        w2b = sb("w2b", [P, D], f32)
        b1b = sb("b1b", [P, D], f32)
        rels = sb("rels", [P, 2, D], f32)
        relT = sb("relT", [P, 2 * P], f32)
        w1a = sb("w1a", [P, D + 1], f32)
        ub = sb("ub", [P, 1], f32)
        relw = sb("relw", [P, 2, D + 1], f32)
        rel3 = sb("rel3", [P, 2, 3, D + 1], bf16)
        junk = sb("junk", [P, D + 1], f32)

        general = sb("general", [P, 1], i32)
        idx_t = sb("idx_t", [P, NK * P], u32)
        plc_t = sb("plc_t", [P, NK * P], f32)
        has_t = sb("has_t", [P, NG], f32)

        xn = sb("xn", [P, 4, GS, D], f32)
        xe = sb("xe", [P, 4, GS, D], f32)
        an = sb("an", [P, 2, BG, D], f32)
        ae = sb("ae", [P, 2, BG, D], f32)
        heT = sb("heT", [P, 2, BG * P], f32)
        hnT = sb("hnT", [P, 2, GS * P], f32)
        cs = sb("cs", [P, 2, GS, D + 2], f32)
        sel = sb("sel", [P, 2, BG, P], f32)
        plr = sb("plr", [P, 2, GS * P], bf16)
        tyr = sb("tyr", [P, 2, GS * P], bf16)
        ota = sb("ota", [P, 2, GS * P], bf16)
        otb = sb("otb", [P, 2, GS * P], bf16)
        selT = sb("selT", [P, 2, GS * P], bf16)
        scn = sb("scn", [GS, 4, 4, P], f32)
        plc = sb("plc", [P, 4, GS], f32)
        idx = sb("idx", [P, 4, GS], u32)
        qc = sb("qc", [P, 2, BG * D], f32)
        lr = sb("lr", [P, 2, BG * D], f32)
        st = sb("st", [P, 2 * GS, 6], f32)
        tiny = sb("tiny", [P, 12, 2 * GS], f32)
        rstd0 = sb("rstd0", [P, 2 * GS], f32)
        lnv = sb("lnv", [P, 2 * GS], f32)
        var = sb("var", [P, 2 * GS], f32)
        rstd = sb("rstd", [P, 2, 2 * GS], f32)
        nbias = sb("nbias", [P, 2, 2 * GS], f32)
        sn3 = sb("sn3", [P, GS, 3], bf16)
        snr = sb("snr", [P, 2, GS], f32)
        sc = sb("sc", [P, 3, GS], f32)
        rows = sb("rows", [P, 8, P], f32)
        alpha = sb("alpha", [P, 2, GS], f32)
        half = sb("half", [P, GS, 64], bf16)[:, :, :]
        quarter = sb("quarter", [P, GS, 32], bf16)[:, :, :]
        some = sb("some", [P, 2, GS, 16], bf16)

        tn_p = pb("tn_p", [P, BG * P], f32)
        te_p = pb("te_p", [P, 2, BG * P], f32)
        c_p = pb("c_p", [P, 2, 512], f32)
        y_p = pb("y_p", [P, 2, BG * D], f32)
        s_p = pb("s_p", [P, 512], f32)
        sd_p = s_p[:, 0:3 * GS]
        bT_p, alT_p = s_p[0:GS, 64:64 + P], s_p[:, 192:192 + GS]

        k_in = sem("k_in")
        k_const = sem("k_const")
        k_pool = sem("k_pool")
        k_dve = sem("k_dve")
        k_pe = sem("k_pe")
        k_start = sem("k_start")
        k_startl = sem("k_startl")
        k_gat = [sem(f"k_gat{i}") for i in range(2)]
        k_free = sem("k_free")
        k_idx = sem("k_idx")
        k_tr = sem("k_tr")
        k_out = [sem(f"k_out{i}") for i in range(2)]
        k_rows = sem("k_rows")

        with ExitStack() as ctx1:
            dsti = xn[:, 0, 0:4, :].rearrange("p a b -> p (a b)")[:, 0:EC].bitcast(i32)
            hi_i = xn[:, 0, 4:8, :].rearrange("p a b -> p (a b)")[:, 0:EC].bitcast(i32)
            lo_i = xn[:, 0, 8:12, :].rearrange("p a b -> p (a b)")[:, 0:EC].bitcast(i32)
            hi_f = xn[:, 1, 0:4, :].rearrange("p a b -> p (a b)")[:, 0:EC]
            lo_f = xn[:, 1, 4:8, :].rearrange("p a b -> p (a b)")[:, 0:EC]
            CH = EC // 4
            oh_h = hnT[:, :, :].rearrange("p a b -> p (a b)").bitcast(bf16)[:, 0:CH * 32].rearrange("p (c h) -> p c h", h=32)
            oh_l = cs[:, 0, :, :].rearrange("p a b -> p (a b)").bitcast(bf16)[:, 0:CH * 32].rearrange("p (c h) -> p c h", h=32)
            hist_p = tn_p[:, 0:P]
            cnt_p = tn_p[0:32, 128:160]
            pre_p = tn_p[0:32, 160:161]
            histm = sel[:, 0, 0, :]
            histr = sel[:, 0, 1, 0:32]
            cnt = sel[0:32, 0, 2, 0:32]
            cum = sel[0:32, 0, 2, 32:64]
            pre = sel[0:32, 0, 2, 64:65]
            zero32 = sel[0:32, 0, 2, 96:128]
            sta = sel[0:32, 0, 3, 0:32]
            stai = sel[0:32, 0, 3, 32:64].bitcast(i32)
            first = lr[:, 0, 0:NK].bitcast(i32)
            gd = [xe[:, i, 0, :].bitcast(i32) for i in range(2)]
            gs_ = [xe[:, i, 1, :].bitcast(i32) for i in range(2)]
            gt = [xe[:, i, 2, :].bitcast(i32) for i in range(2)]
            plf = [xe[:, i, 3, :] for i in range(2)]
            idf = [xe[:, i, 4, :] for i in range(2)]
            srf = [xe[:, i, 5, :] for i in range(2)]
            mf = [xe[:, i, 6:10, :] for i in range(2)]
            plb = [xe[:, i, 10, 0:64].bitcast(bf16) for i in range(2)]
            tyb = [xe[:, i, 11, 0:64].bitcast(bf16) for i in range(2)]

            block = ctx1.enter_context(nc.Block())
            NIN = 7
            nextp = alpha[:, 0, 0:1].bitcast(i32)
            bad = alpha[:, 0, 2:4]
            number = lr[0:32, 1, 0:32]
            badf = alpha[0:1, 0, 4:5]
            wrong = xn[:, 2, 0:4, :].rearrange("p a b -> p (a b)")[:, 0:EC]
            flag_p = tn_p[0:1, 192:193]

            @block.sync
            def _(sp):
                sp.dma_start(dsti, dst_e.rearrange("o (p c) -> (o p) c", p=P)).then_inc(k_in, 16)
                sp.wait_ge(k_const, 1)
                sp.dma_start(nextp[0:P - 1, :], dst_e[:, EC:].rearrange("o (p c) -> (o p) c", c=EC)[:, 0:1],
                             allow_slow_non_contiguous=True).then_inc(k_in, 16)
                sp.dma_start(w1s[:, :, :], w1.rearrange("(a p) d -> p a d", p=P)).then_inc(k_in, 16)
                sp.dma_start(rels[:, 0, :], rel[0:P, :]).then_inc(k_in, 16)
                sp.dma_start(rels[0:RB, 1, :], rel[P:R, :]).then_inc(k_in, 16)
                sp.dma_start(w2b[:, :], w2.partition_broadcast(P)).then_inc(k_in, 16)
                sp.dma_start(b1b[:, :], b1.partition_broadcast(P)).then_inc(k_in, 16)
                sp.wait_ge(k_start, 1)
                sp.dma_start(starts_d.rearrange("(h l) o -> h (l o)", l=32), stai).then_inc(k_startl, 16)
                sp.wait_ge(k_startl, 16)
                sp.dma_start(first, starts_d[0:NK * P, :].rearrange("(k p) o -> p (k o)", p=P),
                             allow_slow_non_contiguous=True).then_inc(k_startl, 16)
                for k in range(NK):
                    sp.wait_ge(k_rows, k + 1)
                    for table, made in ((scan_d, mf[k % 2].rearrange("p a b -> p (a b)")), (place_d, plb[k % 2]), (types_d, tyb[k % 2])):
                        sp.dma_start(table[k * P:(k + 1) * P, :], made).then_inc(k_out[k % 2], 16)
                for i in range(2):
                    sp.wait_ge(k_out[i], 48 * ((NK + 1 - i) // 2))

            @block.gpsimd
            def _(pool):
                g = nc.gpsimd
                steps = Steps(pool, k_pool, 0)
                g.iota(row[:, :], pattern=[[1, P]], base=0, channel_multiplier=0, allow_small_or_imprecise_dtypes=True)
                g.iota(row32[:, :], pattern=[[1, 32]], base=0, channel_multiplier=0, allow_small_or_imprecise_dtypes=True)
                g.iota(col[:, :], pattern=[[P, 2]], base=0, channel_multiplier=1, allow_small_or_imprecise_dtypes=True)
                g.iota(gbase[:, :], pattern=[[P * P, NK]], base=0, channel_multiplier=P, allow_small_or_imprecise_dtypes=True)
                g.memset(ident[:, :], 0.0)
                g.memset(ones[:, :], 1.0)
                g.memset(fold[:, :], 0.0)
                g.memset(below[:, :], 1.0)
                steps.then(g.memset(blocks4[:, :], 1.0))
                g.affine_select(out=ident[:, :], in_=ident[:, :], compare_op=ALU.not_equal, fill=1.0, base=0,
                                pattern=[[-1, P]], channel_multiplier=1)
                g.affine_select(out=below[:, :], in_=below[:, :], compare_op=ALU.is_gt, fill=0.0, base=0,
                                pattern=[[1, 32]], channel_multiplier=-1)
                steps.then(g.affine_select(out=blocks4[:, :], in_=blocks4[:, :], compare_op=ALU.is_ge, fill=0.0, base=0,
                                           pattern=[[-32, 4]], channel_multiplier=1))
                steps.then(g.affine_select(out=blocks4[:, :], in_=blocks4[:, :], compare_op=ALU.is_ge, fill=0.0, base=31,
                                           pattern=[[32, 4]], channel_multiplier=-1))
                for a in range(4):
                    steps.then(g.affine_select(out=fold[:, :], in_=fold[:, :], compare_op=ALU.not_equal, fill=1.0,
                                               base=-32 * a, pattern=[[-1, 32]], channel_multiplier=1))
                g.iota(number, pattern=[[1, 32]], base=0, channel_multiplier=32, allow_small_or_imprecise_dtypes=True)
                g.memset(nextp, 2 * N)
                g.memset(bad, 0.0)
                g.memset(zero32, 0.0).then_inc(k_const, 1)
                pool.wait_ge(k_startl, 32)
                for k in range(NK):
                    wait(pool, k_free, k - 1)
                    for to, e in ((gs_, src_e), (gd, dst_e), (gt, typ_e)):
                        g.indirect_dma_start(out=to[k % 2], out_offset=None, in_=e,
                                             in_offset=bass.IndirectOffsetOnAxis(ap=first[:, k:k + 1].bitcast(u32), axis=1)
                                             ).then_inc(k_gat[k % 2], 16)

            @block.tensor
            def _(pe):
                pe.wait_ge(k_const, 1)
                pe.wait_ge(k_in, 16 * NIN)
                nc.tensor.transpose(te_p[:, 0, 0:P], rels[:, 0, :], ident[:, :])
                nc.tensor.transpose(te_p[:, 0, P:P + RB], rels[0:RB, 1, :], ident[0:RB, 0:RB]).then_inc(k_pe, 1)
                for c in range(4):
                    pe.wait_ge(k_idx, c + 1)
                    for j in range(CH // 4 + (CH % 4 > 0)):
                        w = min(4, CH - 4 * j)
                        last = nc.tensor.matmul(hist_p[0:32 * w, 0:32 * w],
                                                oh_h[:, 4 * j:4 * j + w, :].rearrange("p c h -> p (c h)"),
                                                oh_l[:, 4 * j:4 * j + w, :].rearrange("p c h -> p (c h)"),
                                                start=(c == 0 and j == 0), stop=(c == 3 and 4 * j + w == CH),
                                                skip_group_check=True)
                    last.then_inc(k_tr, 1)
                pe.wait_ge(k_idx, 5)
                nc.tensor.matmul(cnt_p, fold[:, :], histr, start=True, stop=True).then_inc(k_tr, 1)
                pe.wait_ge(k_idx, 6)
                nc.tensor.matmul(pre_p, below[:, :], cum[:, 31:32], start=True, stop=True).then_inc(k_tr, 1)
                pe.wait_ge(k_idx, 7)
                nc.tensor.matmul(flag_p, bad[:, 0:1], ones[:, :], start=True, stop=False)
                nc.tensor.matmul(flag_p, bad[:, 1:2], ones[:, :], start=False, stop=True)
                nc.tensor.matmul(te_p[:, 1, 0:P], relT[:, 0:P], w1s[:, 2, :], start=True, stop=True)
                nc.tensor.matmul(te_p[0:RB, 1, P:2 * P], relT[:, P:P + RB], w1s[:, 2, :], start=True, stop=True).then_inc(k_tr, 1)
                for k in range(NK):
                    pe.wait_ge(k_rows, k + 1)
                    wait(pe, k_free, k - 1)
                    nc.tensor.transpose(c_p[:, k % 2, 0:P], idf[k % 2], ident[:, :])
                    nc.tensor.transpose(c_p[:, k % 2, P:2 * P], plf[k % 2], ident[:, :]).then_inc(k_pe, 1)

            @block.vector
            def _(dve):
                v = nc.vector
                steps = Steps(dve, k_dve, 0)
                dve.wait_ge(k_in, 16 * NIN)
                dve.wait_ge(k_const, 1)
                v.tensor_scalar(hi_i, dsti, 12, None, ALU.logical_shift_right)
                steps.then(v.tensor_scalar(lo_i, dsti, 20, 27, ALU.logical_shift_left, ALU.logical_shift_right))
                v.tensor_copy(hi_f, hi_i)
                steps.then(v.tensor_copy(lo_f, lo_i))
                for c in range(4):
                    wait(dve, k_tr, c)
                    r32 = row32[:, :].unsqueeze(1).to_broadcast([P, CH, 32])
                    v.tensor_tensor(oh_h, hi_f[:, c * CH:(c + 1) * CH].unsqueeze(2).to_broadcast([P, CH, 32]), r32, ALU.is_equal)
                    v.tensor_tensor(oh_l, lo_f[:, c * CH:(c + 1) * CH].unsqueeze(2).to_broadcast([P, CH, 32]), r32,
                                    ALU.is_equal).then_inc(k_idx, 1)
                dve.wait_ge(k_tr, 4)
                steps.then(v.tensor_tensor(histm.rearrange("p (a l) -> p a l", a=4), hist_p.rearrange("p (a l) -> p a l", a=4),
                                           blocks4[:, :].unsqueeze(2).to_broadcast([P, 4, 32]), ALU.mult))
                v.tensor_reduce(histr, histm.rearrange("p (a l) -> p l a", a=4), AX, ALU.add).then_inc(k_idx, 1)
                dve.wait_ge(k_tr, 5)
                steps.then(v.tensor_copy(cnt, cnt_p))
                v.tensor_tensor_scan(cum, zero32, cnt, 0.0, ALU.add, ALU.add).then_inc(k_idx, 1)
                dve.wait_ge(k_idx, 6)
                dve.wait_ge(k_tr, 6)
                steps.then(v.tensor_copy(pre, pre_p))
                steps.then(v.scalar_tensor_tensor(sta, cum, pre, cnt, ALU.add, ALU.subtract))
                v.tensor_copy(stai, sta).then_inc(k_start, 1)
                v.tensor_tensor(wrong[:, 0:EC - 1], dsti[:, 0:EC - 1], dsti[:, 1:EC], ALU.is_gt)
                v.tensor_tensor(wrong[:, EC - 1:EC], dsti[:, EC - 1:EC], nextp, ALU.is_gt)
                steps.then(v.tensor_scalar(cnt, cnt, float(P), None, ALU.is_gt))
                steps.then(v.scalar_tensor_tensor(cnt, number, float(NG), cnt, ALU.is_lt, ALU.mult))
                v.tensor_reduce(bad[:, 0:1], wrong, AX, ALU.add)
                steps.then(v.tensor_reduce(bad[0:32, 1:2], cnt, AX, ALU.add))
                dve.wait_ge(k_pe, 1)
                v.tensor_copy(relT[:, 0:P + RB], te_p[:, 0, 0:P + RB]).then_inc(k_idx, 1)
                v.tensor_copy(w1a[:, 0:D], w1s[:, 0, :])

                def dot_w2(into, a, n):
                    steps.then(v.tensor_tensor_reduce(out=junk[0:n, 0:D], in0=a, in1=w2b[0:n, :], scale=1.0, scalar=0.0,
                                                      op0=ALU.mult, op1=ALU.add, accum_out=into))

                dot_w2(w1a[:, D:D + 1], w1s[:, 0, :], P)
                dot_w2(ub[:, :], w1s[:, 1, :], P)
                dve.wait_ge(k_tr, 7)
                steps.then(v.tensor_scalar(badf, flag_p, 0.5, None, ALU.is_gt))
                steps.then(v.tensor_copy(general[0:1, 0:1], badf))
                for c, n in ((0, P), (1, RB)):
                    steps.then(v.tensor_tensor(relw[0:n, c, 0:D], te_p[0:n, 1, c * P:c * P + D], b1b[0:n, :], ALU.add))
                    dot_w2(relw[0:n, c, D:D + 1], relw[0:n, c, 0:D], n)
                    steps.then(v.tensor_copy(rel3[0:n, c, 0, :], relw[0:n, c, :]))
                    steps.then(v.tensor_tensor(junk[0:n, :], relw[0:n, c, :], rel3[0:n, c, 0, :], ALU.subtract))
                    steps.then(v.tensor_copy(rel3[0:n, c, 1, :], junk[0:n, :]))
                    steps.then(v.tensor_tensor(rel3[0:n, c, 2, :], junk[0:n, :], rel3[0:n, c, 1, :], ALU.subtract))
                for k in range(NK):
                    i = k % 2
                    dve.wait_ge(k_gat[i], 48 * (k // 2 + 1))
                    wait(dve, k_out[i], 48 * (k // 2))
                    p, m = plf[i], mf[i]
                    v.tensor_copy(srf[i], gs_[i])
                    v.tensor_copy(tyb[i], gt[i])
                    steps.then(v.tensor_copy(p, gd[i]))
                    steps.then(v.tensor_scalar(p, p, gbase[:, k:k + 1], OFF, ALU.subtract, ALU.min))
                    v.tensor_copy(plb[i], p)
                    v.tensor_scalar(idf[i], p, float(P - 1), SKIP, ALU.is_gt, ALU.mult)
                    v.memset(m[:, 2, 0:1], 0.0)
                    v.memset(m[:, 3, P - 1:P], 0.0)
                    v.tensor_tensor(m[:, 2, 1:P], p[:, 1:P], p[:, 0:P - 1], ALU.is_equal)
                    steps.then(v.tensor_tensor(m[:, 3, 0:P - 1], p[:, 0:P - 1], p[:, 1:P], ALU.is_equal))
                    v.tensor_scalar(m[:, 0:2, :], m[:, 2:4, :], 1.0, FAR, ALU.subtract, ALU.mult)
                    v.tensor_tensor(idf[i], idf[i], srf[i], ALU.add).then_inc(k_rows, 1)
                    dve.wait_ge(k_pe, k + 2)
                    v.tensor_copy(idx_t[:, k * P:(k + 1) * P], c_p[:, i, 0:P])
                    v.tensor_copy(plc_t[:, k * P:(k + 1) * P], c_p[:, i, P:2 * P]).then_inc(k_free, 1)
                dve.wait_ge(k_free, NK)
                for i in range(2):
                    dve.wait_ge(k_out[i], 48 * ((NK + 1 - i) // 2))
                v.memset(xe[:, :, :, :], 0.0)
                v.memset(rows[:, :, :], 0.0)
                for i in range(4):
                    last = v.memset(xn[:, i, :, :], 0.0)
                last.then_inc(k_free, 1)

        general_buffers = (ident, w1a, w1s, ub, relw, R, te_p, c_p, y_p, xe, ae, sel, rows, tiny)
        flag = nc.values_load(general[0:1, 0:1], min_val=0, max_val=1, skip_runtime_bounds_check_because="the chip makes it 0 or 1")
        with nc.If(flag == 0), ExitStack() as ctx2:
            L1, L2 = Semaphores(sem, 1), Semaphores(sem, 2)

            block = ctx2.enter_context(nc.Block())

            def nodes_of(a, t, tail):
                if not tail:
                    half = GS // 2
                    return [(a[bass.ds(t.n * GS * P + h * half * P, half * P), :].rearrange("(g p) d -> p g d", p=P),
                             h * half, (h + 1) * half, P) for h in range(2)]
                at = (NSB - 1) * GS * P
                parts = []
                if TG:
                    half = TG // 2
                    for g0, g1 in ((0, half), (half, TG)):
                        parts.append((a[at + g0 * P:at + g1 * P, :].rearrange("(g p) d -> p g d", p=P), g0, g1, P))
                if TR:
                    parts.append((a[at + TG * P:N, :].rearrange("(g p) d -> p g d", p=TR), TG, TG + 1, TR))
                return parts

            NTAIL = 2 + (TR > 0)

            @block.sync
            def _(sp):
                def done(L, n):
                    if L is L1:
                        wait(sp, L1.x1, n)
                    elif not (isinstance(n, int) and n <= 0):
                        sp.wait_ge(L2.yfree, 2 + NBLK * n)

                def load_x(L, a, t, tail=False):
                    wait(sp, L.stored[t.slot4], 32 * t.round4)
                    first, second, *rest = nodes_of(a, t, tail)
                    for r_rows, r0, r1, r_np in rest:
                        sp.dma_start(xn[0:r_np, t.slot4, r0:r1, :], r_rows).then_inc(L.rest_in, 16)
                        sp.wait_ge(L.rest_in, 16)
                    for rows_, g0, g1, np_ in (first, second):
                        sp.dma_start(xn[0:np_, t.slot4, g0:g1, :], rows_).then_inc(L.x_in[t.slot4], 16)

                def load_idx(L, t):
                    wait(sp, L.gathered[t.slot4], 256 * t.round4)
                    sp.dma_start(idx[:, t.slot4, :], idx_t[:, bass.ds(t.n * GS, GS)]).then_inc(L.idx_in[t.slot4], 16)

                def load_rows(L, n, t):
                    done(L, t.n - 3)
                    sp.sem_inc(L.row_turns, 1)
                    sp.dma_start(plc[:, t.slot4, :], plc_t[:, bass.ds(t.n * GS, GS)]).then_inc(L.rows_in[t.slot4], 16)
                    if n == 1:
                        sp.dma_start(scn[:, t.slot4, :, :].rearrange("g a b -> g (a b)"),
                                     scan_d[bass.ds(t.n * GS, GS), :]).then_inc(L.rows_in[t.slot4], 16)

                def load_tables(t):
                    wait(sp, L1.oh, t.n - 1)
                    sp.sem_inc(L1.row_turns, 1)
                    for to, table in ((plr, place_d), (tyr, types_d)):
                        sp.dma_start(to[:, t.slot2, :],
                                     table[bass.ds(t.n * GS, GS), :].rearrange("g s -> (g s)").partition_broadcast(P)
                                     ).then_inc(L1.tables_in[t.slot2], 16)

                def store(L, a, t, tail=False):
                    done(L, t.n + 1)
                    for rows_, g0, g1, np_ in nodes_of(a, t, tail):
                        sp.dma_start(rows_, xn[0:np_, t.slot4, g0:g1, :]).then_inc(L.stored[t.slot4], 16)

                def layer(L, n, a, to):
                    def load(t, tail=False):
                        load_rows(L, n, t)
                        if n == 1:
                            load_tables(t)
                        load_x(L, a, t, tail)

                    def turn(i, k, last=False):
                        if not last or k < 1:
                            load_idx(L, At(i, k + 4))
                        if not last or k < 2:
                            load(At(i, k + 3), tail=last and k == 1)
                        store(L, to, At(i, k))

                    for k in range(4):
                        load_idx(L, At(0, k))
                    for k in range(3):
                        load(At(0, k))
                    for k in range(4):
                        turn(0, k)
                    with nc.sync.Fori(1, LOOPS - 1) as i:
                        for k in range(4):
                            turn(i, k)
                    for k in range(4):
                        turn(LOOPS - 1, k, last=True)
                    store(L, to, At(LOOPS, 0), tail=True)
                    for s in range(4):
                        sp.wait_ge(L.stored[s], 32 * LOOPS + (16 * NTAIL if s == 0 else 0))

                sp.wait_ge(k_free, NK + 1)
                layer(L1, 1, x, x1_d)
                layer(L2, 2, x1_d, out)

            @block.gpsimd
            def _(pool):
                def gather(L, a, t):
                    wait(pool, L.idx_in[t.slot4], 16 * (t.round4 + 1))
                    wait(pool, L.ae, NBLK * (t.n - 3))
                    pool.sem_inc(L.turns, 1)
                    for j in range(GS):
                        nc.gpsimd.indirect_dma_start(out=xe[:, t.slot4, j, :], out_offset=None, in_=a,
                                                     in_offset=bass.IndirectOffsetOnAxis(ap=idx[:, t.slot4, j:j + 1], axis=0),
                                                     bounds_check=last_row, oob_is_err=False).then_inc(L.gathered[t.slot4], 16)

                pool.wait_ge(k_free, NK + 1)
                last_row = nc.gpsimd.to_reg(N - 1)

                def nodes_with_edges(t):
                    pool.wait_ge(L1.oh, t.n + 1)
                    wait(pool, L1.rstd, t.n - 1)
                    pool.sem_inc(L1.has_turns, 1)
                    marks = selT[:, t.slot2, :].rearrange("p (g s) -> p g s", s=P)
                    for level, to in enumerate((half, quarter, some[:, t.slot2, :, :])):
                        n = to.shape[2]
                        nc.gpsimd.tensor_tensor(to, marks[:, :, 0:n], marks[:, :, n:2 * n], ALU.add).then_inc(L1.has, 1)
                        pool.wait_ge(L1.has, 3 * t.n + level + 1)
                        marks = to

                for L, a in ((L1, x), (L2, x1_d)):
                    if L is L2:
                        for s in range(4):
                            pool.wait_ge(L1.stored[s], 32 * LOOPS + (16 * NTAIL if s == 0 else 0))
                    for k in range(5):
                        if L is L1 and k >= 2:
                            nodes_with_edges(At(0, k - 2))
                        gather(L, a, At(0, k))
                    with nc.gpsimd.Fori(1, LOOPS) as i:
                        for k in range(1, 5):
                            if L is L1:
                                nodes_with_edges(At(i, k - 2))
                            gather(L, a, At(i, k))
                    if L is L1:
                        nodes_with_edges(At(LOOPS, -1))
                        nodes_with_edges(At(LOOPS, 0))

            h2 = hnT[:, :, :].rearrange("p s (g d) -> p s g d", g=GS)
            own = cs[:, :, :, 0:D]

            def run(engine_fori, turn):
                turn(At(0, 0), None, None)
                for k in range(4):
                    turn(At(0, k + 1), At(0, k), At(0, k - 1) if k else None)
                with engine_fori(1, LOOPS) as i:
                    for k in range(4):
                        turn(At(i, k + 1), At(i, k), At(i, k - 1))
                turn(None, At(LOOPS, 0), At(LOOPS, -1))
                turn(None, None, At(LOOPS, 0))

            @block.vector
            def _(dve):
                v = nc.vector
                SOFT = 8
                K_FIRST = {1: 9, 2: 7}
                K_SECOND = SOFT + NBLK - 1

                def stats_some(L, t, part):
                    if t is None:
                        return
                    if part == 0:
                        dve.wait_ge(L.x_in[t.slot4], 32 * (t.round4 + 1))
                    if part == 4:
                        dve.wait_ge(L.gathered[t.slot4], 256 * (t.round4 + 1))
                    for j in range(part % 4 * BG, part % 4 * BG + BG):
                        if part < 4:
                            v.bn_stats(st[:, GS + j, :], xn[:, t.slot4, j, :])
                        else:
                            last = v.bn_stats(st[:, j, :], xe[:, t.slot4, j, :])
                    if part == 7:
                        last.then_inc(L.first, 1)

                def variances(L, n, t):
                    if t is None:
                        return
                    steps = Steps(dve, L.first, K_FIRST[n] * t.n)
                    steps.n = 1
                    steps.settle()
                    msum, dm, m2, dm2, m2e = (tiny[:, c, :] for c in range(5))
                    v.tensor_tensor(msum, st[:, :, 1], st[:, :, 4], ALU.add)
                    v.tensor_tensor(dm, st[:, :, 1], st[:, :, 4], ALU.subtract)
                    steps.then(v.tensor_tensor(m2, st[:, :, 2], st[:, :, 5], ALU.add))
                    v.scalar_tensor_tensor(dm2, dm, 0.25, dm, ALU.mult, ALU.mult)
                    steps.then(v.tensor_scalar(m2e, m2, 1.0 / D, EPS, ALU.mult, ALU.add))
                    v.tensor_tensor(var[:, :], dm2, m2e, ALU.add).then_inc(L.var, 1)

                def factors(L, n, t):
                    if t is None:
                        return
                    steps = Steps(dve, L.first, K_FIRST[n] * t.n)
                    steps.n = 3
                    has = has_t[:, bass.ds(t.n * GS, GS)]
                    if n == 1:
                        dve.wait_ge(L.has, 3 * (t.n + 1))
                        steps.then(v.tensor_reduce(has, some[:, t.slot2, :, :], AX, ALU.add))
                        steps.then(v.tensor_scalar(has, has, 0.5, None, ALU.is_gt))
                    dve.wait_ge(L.rstd0, t.n + 1)
                    msum, t0, t1 = tiny[:, 0, :], tiny[:, 5, :], tiny[:, 6, :]
                    r = rstd[:, t.slot2, :]
                    steps.then(v.tensor_tensor(t0, var[:, :], rstd0[:, :], ALU.mult))
                    steps.then(v.scalar_tensor_tensor(t1, t0, -0.5, rstd0[:, :], ALU.mult, ALU.mult))
                    wait(dve, L.ae, NBLK * (t.n - 1))
                    wait(dve, L.an, NBLK * (t.n - 1))
                    if n == 2:
                        v.tensor_scalar(tiny[:, 7, 0:GS], has, -1.0, 1.0, ALU.mult, ALU.add)
                        has = tiny[:, 7, 0:GS]
                    steps.then(v.scalar_tensor_tensor(r, t1, 1.5, rstd0[:, :], ALU.add, ALU.mult))
                    steps.then(v.tensor_tensor(r[:, GS:2 * GS], r[:, GS:2 * GS], has, ALU.mult))
                    v.scalar_tensor_tensor(nbias[:, t.slot2, :], msum, -0.5, r, ALU.mult, ALU.mult).then_inc(L.rstd, 1)
                    assert steps.n == K_FIRST[n], steps.n

                def one_hots(t):
                    if t is None:
                        return
                    L = L1
                    dve.wait_ge(L.tables_in[t.slot2], 32 * (t.round2 + 1))
                    wait(dve, L.sd, t.n - 1)
                    wait(dve, L.c, NBLK * (t.n - 1))
                    wait(dve, L.has, 3 * (t.n - 1))
                    v.tensor_scalar(ota[:, t.slot2, :], tyr[:, t.slot2, :], col[:, 0:1], None, ALU.is_equal)
                    v.tensor_scalar(otb[:, t.slot2, :], tyr[:, t.slot2, :], col[:, 1:2], None, ALU.is_equal)
                    v.tensor_scalar(selT[:, t.slot2, :], plr[:, t.slot2, :], col[:, 0:1], None, ALU.is_equal).then_inc(L.oh, 1)

                def split_scores(t):
                    if t is None:
                        return
                    steps = Steps(dve, L1.split, 3 * t.n)
                    sn = cs[:, t.slot2, :, D + 1]
                    dve.wait_ge(L1.cs, NBLK * (t.n + 1))
                    steps.then(v.tensor_copy(sn3[:, :, 0], sn))
                    steps.then(v.tensor_tensor(snr[:, 0, :], sn, sn3[:, :, 0], ALU.subtract))
                    steps.then(v.tensor_copy(sn3[:, :, 1], snr[:, 0, :]))
                    v.tensor_tensor(sn3[:, :, 2], snr[:, 0, :], sn3[:, :, 1], ALU.subtract).then_inc(L1.sn3, 1)

                mF, mB, d, w, sF, sB, rc, al = (rows[0:GS, c, :] for c in range(8))

                def scores(m, steps):
                    L = L1
                    sd, b0, b = sc[:, 0, :], sc[:, 1, :], sc[:, 2, :]
                    dve.wait_ge(L.sd, m.n + 1)
                    dve.wait_ge(L.cs, NBLK * (m.n + 1))
                    steps.then(v.tensor_reduce(sd, sd_p.rearrange("p (g a) -> p g a", a=3), AX, ALU.add))
                    steps.then(v.tensor_tensor(b0, sd, cs[:, m.slot2, :, D], ALU.add))
                    v.scalar_tensor_tensor(b, b0, SLOPE, b0, ALU.mult, ALU.max).then_inc(L.b, 1)

                def maxima(m, steps):
                    dve.wait_ge(L1.rows_in[m.slot4], 32 * (m.round4 + 1))
                    dve.wait_ge(L1.bT, m.n + 1)
                    reset = scn[:, m.slot4, :, :]
                    steps.then(v.tensor_tensor_scan(mF, reset[:, 0, :], bT_p, -FAR, ALU.add, ALU.max))
                    steps.then(v.tensor_tensor_scan(mB[:, ::-1], reset[:, 1, ::-1], mF[:, ::-1], -FAR, ALU.add, ALU.max))
                    v.tensor_tensor(d, bT_p, mB, ALU.subtract).then_inc(L1.d, 1)

                def weights(m, steps):
                    dve.wait_ge(L1.w, m.n + 1)
                    reset = scn[:, m.slot4, :, :]
                    steps.then(v.tensor_tensor_scan(sF, reset[:, 2, :], w, 0.0, ALU.mult, ALU.add))
                    steps.then(v.tensor_tensor_scan(sB[:, ::-1], reset[:, 3, ::-1], sF[:, ::-1], 0.0, ALU.mult, ALU.max))
                    steps.then(v.reciprocal(rc, sB))
                    v.tensor_tensor(al, w, rc, ALU.mult).then_inc(L1.al, 1)

                def select(L, m, q):
                    if q >= 2:
                        dve.wait_ge(L.y, NBLK * m.n + q - 1)
                    for j in range(BG):
                        g = q * BG + j
                        if L is L1:
                            last = v.tensor_scalar(sel[:, q % 2, j, :], row[:, :], plc[:, m.slot4, g:g + 1],
                                                   alpha[:, 0, g:g + 1], ALU.is_equal, ALU.mult)
                        else:
                            last = v.tensor_scalar(sel[:, q % 2, j, :], row[:, :], plc[:, m.slot4, g:g + 1], None,
                                                   ALU.is_equal)
                    last.then_inc(L.sel, 1)

                def add1(m, f, steps):
                    L = L1
                    dve.wait_ge(L.qc, NBLK * m.n + f + 1)
                    if f == 1:
                        wait(dve, L.x1, m.n)
                    elif f >= 2:
                        dve.wait_ge(L.second, steps.done + SOFT + f - 1)
                    v.tensor_tensor(lr[:, f % 2, :], y_p[:, f % 2, :], qc[:, f % 2, :], ALU.max).then_inc(L.yfree, 1)
                    dve.wait_ge(L.yfree, 2 + NBLK * m.n + f + 1)
                    xs = xn[:, m.slot4, f * BG:(f + 1) * BG, :].rearrange("p a b -> p (a b)")
                    last = v.tensor_tensor(xs, xs, lr[:, f % 2, :], ALU.add)
                    if f < NBLK - 1:
                        steps.mark(last)
                    else:
                        last.then_inc(L.x1, 1)

                def turn1(n, t, m):
                    L = L1
                    if m is None:
                        one_hots(n)
                        for part in range(8):
                            stats_some(L, n, part)
                        variances(L, 1, n)
                        factors(L, 1, n)
                        split_scores(t)
                        return
                    steps = Steps(dve, L.second, K_SECOND * m.n)
                    scores(m, steps)
                    stats_some(L, n, 0)
                    maxima(m, steps)
                    stats_some(L, n, 1)
                    weights(m, steps)
                    one_hots(n)
                    dve.wait_ge(L.alT, m.n + 1)
                    steps.then(v.tensor_copy(alpha[:, 0, :], alT_p))
                    select(L, m, 0)
                    select(L, m, 1)
                    stats_some(L, n, 2)
                    add1(m, 0, steps)
                    select(L, m, 2)
                    stats_some(L, n, 3)
                    stats_some(L, n, 4)
                    add1(m, 1, steps)
                    select(L, m, 3)
                    for part in range(5, 8):
                        stats_some(L, n, part)
                    variances(L, 1, n)
                    add1(m, 2, steps)
                    factors(L, 1, n)
                    split_scores(t)
                    add1(m, 3, steps)
                    assert steps.n == K_SECOND, steps.n

                def own_row(m, q):
                    dve.wait_ge(L2.an, NBLK * m.n + q + 1)
                    xs = xn[:, m.slot4, q * BG:(q + 1) * BG, :]
                    v.tensor_tensor(xs, xs, own[:, m.slot2, q * BG:(q + 1) * BG, :], ALU.add).then_inc(L2.second, 1)

                def add2(m, f):
                    dve.wait_ge(L2.second, NBLK * m.n + f + 1)
                    dve.wait_ge(L2.y, NBLK * m.n + f + 1)
                    xs = xn[:, m.slot4, f * BG:(f + 1) * BG, :].rearrange("p a b -> p (a b)")
                    v.tensor_tensor(xs, xs, y_p[:, f % 2, :], ALU.add).then_inc(L2.yfree, 1)

                def turn2(n, t, m):
                    L = L2
                    if m is None:
                        for part in range(8):
                            stats_some(L, n, part)
                        variances(L, 2, n)
                        factors(L, 2, n)
                        return
                    dve.wait_ge(L.rows_in[m.slot4], 16 * (m.round4 + 1))
                    select(L, m, 0)
                    select(L, m, 1)
                    for q in range(NBLK):
                        own_row(m, q)
                        stats_some(L, n, 2 * q)
                        if q >= 2:
                            select(L, m, q)
                        if q > 0:
                            add2(m, q - 1)
                        stats_some(L, n, 2 * q + 1)
                    variances(L, 2, n)
                    add2(m, NBLK - 1)
                    factors(L, 2, n)

                dve.wait_ge(k_free, NK + 1)
                v.memset(alpha[:, 1, 0:1], 0.0).then_inc(L1.yfree, 2)
                v.memset(alpha[:, 1, 1:2], 0.0).then_inc(L2.yfree, 2)
                run(v.Fori, turn1)
                dve.wait_ge(L1.second, K_SECOND * NSB)
                run(v.Fori, turn2)

            @block.scalar
            def _(act):
                a = nc.scalar.activation

                def inverse_roots(L, t):
                    if t is None:
                        return
                    act.wait_ge(L.var, t.n + 1)
                    a(lnv[:, :], var[:, :], ACT.Ln).then_inc(L.ln, 1)
                    act.wait_ge(L.ln, t.n + 1)
                    a(rstd0[:, :], lnv[:, :], ACT.Exp, scale=-0.5).then_inc(L.rstd0, 1)

                def norm(L, t, q, function, to, rows_, base, signal):
                    for j in range(BG):
                        g = q * BG + j
                        last = a(to[:, j, :], rows_[:, g, :], function, bias=nbias[:, t.slot2, base + g:base + g + 1],
                                 scale=rstd[:, t.slot2, base + g:base + g + 1])
                    last.then_inc(signal, 1)

                def exponentials(m):
                    act.wait_ge(L1.d, m.n + 1)
                    a(rows[0:GS, 3, :], rows[0:GS, 2, :], ACT.Exp).then_inc(L1.w, 1)

                def messages_out(t, q):
                    act.wait_ge(L1.c, NBLK * t.n + q + 1)
                    if q == 0:
                        wait(act, L1.y, NBLK * (t.n - 1))
                    a(cs[:, t.slot2, q * BG:(q + 1) * BG, :].rearrange("p (a b) c -> p a (b c)", a=2),
                      c_p[:, :, 0:2 * (D + 2)], ACT.Copy).then_inc(L1.cs, 1)

                def slopes(m, q):
                    act.wait_ge(L1.y, NBLK * m.n + q + 1)
                    act.wait_ge(L1.yfree, NBLK * m.n + q + 1)
                    a(qc[:, q % 2, :], y_p[:, q % 2, :], ACT.Copy, scale=SLOPE).then_inc(L1.qc, 1)

                def normed(t, q):
                    if t is None:
                        return
                    L = L1
                    if q == 0:
                        act.wait_ge(L.rstd, t.n + 1)
                    wait(act, L.tn, NBLK * t.n + q - 1)
                    norm(L, t, q, ACT.Identity, an[:, q % 2, :, :], xn[:, t.slot4, :, :], GS, L.an)
                    wait(act, L.te, NBLK * t.n + q - 1)
                    norm(L, t, q, ACT.Identity, ae[:, q % 2, :, :], xe[:, t.slot4, :, :], 0, L.ae)

                def turn1(n, t, m):
                    L = L1
                    if t is None and m is not None:
                        exponentials(m)
                    for q in range(NBLK):
                        if t is not None:
                            act.wait_ge(L.tn, NBLK * t.n + q + 1)
                            wait(act, L.y, NBLK * (t.n - 1))
                            a(hnT[:, t.slot2, q * BG * P:(q + 1) * BG * P], tn_p[:, :], ACT.Relu).then_inc(L.hn, 1)
                            act.wait_ge(L.te, NBLK * t.n + q + 1)
                            wait(act, L.c, NBLK * t.n + q - 1)
                            a(heT[:, q % 2, :], te_p[:, q % 2, :], ACT.Relu).then_inc(L.he, 1)
                            if q == 0 and m is not None:
                                exponentials(m)
                        if q > 0 and m is not None:
                            slopes(m, q - 1)
                        if t is not None and q < NBLK - 1:
                            normed(t, q + 1)
                        if q == NBLK - 1:
                            inverse_roots(L, n)
                        if t is not None:
                            messages_out(t, q)
                    if m is not None:
                        slopes(m, NBLK - 1)
                    normed(n, 0)

                def turn2(n, t, m):
                    L = L2
                    if t is not None:
                        act.wait_ge(L.rstd, t.n + 1)
                        wait(act, L.y, NBLK * (t.n - 1))
                        wait(act, L.second, NBLK * (t.n - 1))
                        for q in range(NBLK):
                            norm(L, t, q, ACT.Relu, own[:, t.slot2, q * BG:(q + 1) * BG, :], xn[:, t.slot4, :, :], GS, L.an)
                            norm(L, t, q, ACT.Relu, h2[:, t.slot2, q * BG:(q + 1) * BG, :], xe[:, t.slot4, :, :], 0, L.ae)
                    inverse_roots(L, n)

                nc.scalar.preload_act_table_set("natural_log_exp_and_others")
                run(nc.scalar.Fori, turn1)
                run(nc.scalar.Fori, turn2)

            @block.tensor
            def _(pe):
                mm, tr = nc.tensor.matmul, nc.tensor.transpose

                def messages(t, q):
                    L = L1
                    pe.wait_ge(L.he, NBLK * t.n + q + 1)
                    pe.wait_ge(L.hn, NBLK * t.n + q + 1)
                    pe.wait_ge(L.oh, t.n + 1)
                    wait(pe, L.cs, NBLK * t.n + q)
                    for j in range(BG):
                        s = slice((q * BG + j) * P, (q * BG + j + 1) * P)
                        at = j % 2 * (D + 2)
                        to = c_p[:, j // 2, at:at + D + 1]
                        mm(to, heT[:, q % 2, j * P:(j + 1) * P], w1a[:, :], start=True, stop=False)
                        for part in range(3):
                            mm(to, ota[:, t.slot2, s], rel3[:, 0, part, :], start=False, stop=False)
                        for part in range(3):
                            mm(to, otb[0:RB, t.slot2, s], rel3[0:RB, 1, part, :], start=False, stop=part == 2)
                        last = mm(c_p[:, j // 2, at + D + 1:at + D + 2], hnT[:, t.slot2, s], ub[:, :], start=True, stop=True)
                    last.then_inc(L.c, 1)

                def aggregate1(m, q):
                    L = L1
                    pe.wait_ge(L.sel, NBLK * m.n + q + 1)
                    pe.wait_ge(L.yfree, NBLK * m.n + q + 1)
                    for j in range(BG):
                        g = q * BG + j
                        to = y_p[:, q % 2, j * D:(j + 1) * D]
                        mm(to, hnT[:, m.slot2, g * P:(g + 1) * P], w1s[:, 1, :], start=True, stop=False)
                        last = mm(to, sel[:, q % 2, j, :], cs[:, m.slot2, g, 0:D], start=False, stop=True)
                    last.then_inc(L.y, 1)

                def scores_to_rows(m):
                    pe.wait_ge(L1.b, m.n + 1)
                    tr(bT_p, sc[:, 2, :], ident[:, :]).then_inc(L1.bT, 1)

                def weights_to_columns(m):
                    pe.wait_ge(L1.al, m.n + 1)
                    mm(alT_p, rows[:, 7, :], ident[:, 0:GS], start=True, stop=True).then_inc(L1.alT, 1)

                def destination_scores(t):
                    L = L1
                    pe.wait_ge(L.sn3, t.n + 1)
                    wait(pe, L.b, t.n)
                    for g in range(GS):
                        last = mm(sd_p[:, 3 * g:3 * g + 3], selT[:, t.slot2, g * P:(g + 1) * P], sn3[:, g, :], start=True, stop=True)
                    last.then_inc(L.sd, 1)

                def nodes_turned(t, q):
                    pe.wait_ge(L1.an, NBLK * t.n + q + 1)
                    wait(pe, L1.hn, NBLK * t.n + q)
                    for j in range(BG):
                        last = tr(tn_p[:, j * P:(j + 1) * P], an[:, q % 2, j, :], ident[:, :])
                    last.then_inc(L1.tn, 1)

                def edges_turned(t, q):
                    pe.wait_ge(L1.ae, NBLK * t.n + q + 1)
                    wait(pe, L1.he, NBLK * t.n + q - 1)
                    for j in range(BG):
                        last = tr(te_p[:, q % 2, j * P:(j + 1) * P], ae[:, q % 2, j, :], ident[:, :])
                    last.then_inc(L1.te, 1)

                def turn1(n, t, m):
                    if m is not None:
                        scores_to_rows(m)
                    if t is None and m is not None:
                        weights_to_columns(m)
                    for q in range(NBLK):
                        if t is not None:
                            messages(t, q)
                            if q == 0 and m is not None:
                                weights_to_columns(m)
                            if q < NBLK - 1:
                                nodes_turned(t, q + 1)
                                edges_turned(t, q + 1)
                        if m is not None:
                            aggregate1(m, q)
                    if t is not None:
                        destination_scores(t)
                    if n is not None:
                        nodes_turned(n, 0)
                        edges_turned(n, 0)

                def turn2(n, t, m):
                    L = L2
                    if m is None:
                        return
                    for q in range(NBLK):
                        pe.wait_ge(L.ae, NBLK * m.n + q + 1)
                        pe.wait_ge(L.sel, NBLK * m.n + q + 1)
                        pe.wait_ge(L.yfree, NBLK * m.n + q + 1)
                        for j in range(BG):
                            last = mm(y_p[:, q % 2, j * D:(j + 1) * D], sel[:, q % 2, j, :], h2[:, m.slot2, q * BG + j, :],
                                      start=True, stop=True)
                        last.then_inc(L.y, 1)

                run(nc.tensor.Fori, turn1)
                run(nc.tensor.Fori, turn2)

        with nc.Else(), ExitStack() as ctx3:
            general_path(nc, ctx3, sem, general_buffers, x, src_e, dst_e, typ_e, out)


def kernel(x, src, dst, edge_type_200, L0_gnn_relation_embedding, L0_gnn_W1, L0_gnn_b1, L0_gnn_w2):
    import numpy as np
    import concourse.bacc as bacc
    from concourse.bass_utils import run_bass_kernel_spmd

    nc = bacc.Bacc("TRN2", target_bir_lowering=False, num_devices=1)
    n_edges, n_nodes = src.shape[0], x.shape[0]
    width = -(-(n_edges + P) // (4 * P)) * 4 * P

    def padded(a, end):
        return np.concatenate([a, np.full(width - n_edges, end, a.dtype)]).reshape(1, width)

    arrays = {"x": np.ascontiguousarray(x), "src": padded(src, 0), "dst": padded(dst, 2 * n_nodes),
              "typ": padded(edge_type_200, 0), "rel": np.ascontiguousarray(L0_gnn_relation_embedding),
              "w1": np.ascontiguousarray(L0_gnn_W1), "b1": np.ascontiguousarray(L0_gnn_b1), "w2": np.ascontiguousarray(L0_gnn_w2)}
    args = [nc.dram_tensor(f"in_{k}", a.shape, mybir.dt.from_np(a.dtype), kind="ExternalInput").ap() for k, a in arrays.items()]
    out = nc.dram_tensor("out", x.shape, mybir.dt.float32, kind="ExternalOutput").ap()
    gnn_two_layers(nc, *args, out)
    r = run_bass_kernel_spmd(nc, [{f"in_{k}": a for k, a in arrays.items()}], core_ids=[0])
    return r.results[0]["out"]
```
